# Optimizing a Trainium2 kernel written in Bass

```python
import numpy as np
import jax
import jax.numpy as jnp

def _softmax(x, axis=-1):
    return jax.nn.softmax(x, axis=axis)

def _gelu(x):
    return jax.nn.gelu(x, approximate=True)

def _silu(x):
    return jax.nn.silu(x)

def _sigmoid(x):
    return jax.nn.sigmoid(x)

def _layernorm(x, axis=-1, eps=1e-05):
    m = jnp.mean(x, axis=axis, keepdims=True)
    v = jnp.var(x, axis=axis, keepdims=True)
    return (x - m) / jnp.sqrt(v + eps)

def _scatter_add(tgt, idx, src, axis=0):
    return tgt.at[idx].add(src)

def _segment_sum(src, seg, n):
    return jax.ops.segment_sum(src, seg, n)
kernel_name = 'mk_gnn_preln_d1_gnn_r8_425aab'

def setup_inputs(seed: int=0):
    np.random.seed(seed)
    _w = jnp.asarray

    def _rec_inputs():
        import jax
        import jax.numpy as jnp
        _gk = jax.random.key(seed)
        x = -0.000202 + 1 * jax.random.normal(jax.random.fold_in(_gk, 1), (12500, 128), jnp.float32)
        _s = jax.random.randint(jax.random.fold_in(_gk, 2), (100000,), 0, 12500, jnp.int32)
        _d = jax.random.randint(jax.random.fold_in(_gk, 3), (100000,), 0, 12500, jnp.int32)
        _loop = jnp.arange(12500, dtype=jnp.int32)
        src = jnp.concatenate([_s, _d, _loop])
        dst = jnp.concatenate([_d, _s, _loop])
        _o = jnp.argsort(dst, stable=True)
        src = src[_o]
        dst = dst[_o]
        edge_attr_16 = 0.000254156 + 0.999948 * jax.random.normal(jax.random.fold_in(_gk, 11), (212500, 16), jnp.float32)
        return (x, src, dst, edge_attr_16)
    x, src, dst, edge_attr_16 = _rec_inputs()

    def _L0_gnn_setup():
        import jax, jax.numpy as jnp
        import numpy as np
        N, E = (6250, 100000)
        D, ED, L = (128, 16, 3)
        key = jax.random.key(seed)
        ks = jax.random.split(key, 16)
        inp = {'x': jax.random.normal(ks[0], (N, D), jnp.float32), 'edge_index': jax.random.randint(ks[1], (2, E), 0, N, jnp.int64), 'edge_attr': jax.random.normal(ks[2], (E, ED), jnp.float32), 'enc_w': jax.random.normal(ks[3], (D, D), jnp.float32) / np.sqrt(D), 'enc_b': jnp.zeros((D,), jnp.float32), 'edge_w': jax.random.normal(ks[4], (L, ED, D), jnp.float32) / np.sqrt(ED), 'edge_b': jnp.zeros((L, D), jnp.float32), 'mlp_w1': jax.random.normal(ks[5], (L, D, 2 * D), jnp.float32) / np.sqrt(D), 'mlp_b1': jnp.zeros((L, 2 * D), jnp.float32), 'mlp_w2': jax.random.normal(ks[6], (L, 2 * D, D), jnp.float32) / np.sqrt(2 * D), 'mlp_b2': jnp.zeros((L, D), jnp.float32), 'eps': jnp.zeros((L,), jnp.float32), 'out_w': jax.random.normal(ks[7], (D * (L + 1), D), jnp.float32) / np.sqrt(D * (L + 1)), 'out_b': jnp.zeros((D,), jnp.float32)}
        return inp
    _L0_gnn_all = _L0_gnn_setup()
    _L0_gnn_in = {k: v for k, v in _L0_gnn_all.items() if k in ('enc_w', 'enc_b', 'edge_w', 'edge_b', 'mlp_w1', 'mlp_b1', 'mlp_w2', 'mlp_b2', 'eps', 'out_w', 'out_b')}
    del _L0_gnn_all
    return {'x': x, 'src': src, 'dst': dst, 'edge_attr_16': edge_attr_16, 'L0_gnn_enc_w': _L0_gnn_in['enc_w'], 'L0_gnn_enc_b': _L0_gnn_in['enc_b'], 'L0_gnn_edge_w': _L0_gnn_in['edge_w'], 'L0_gnn_edge_b': _L0_gnn_in['edge_b'], 'L0_gnn_mlp_w1': _L0_gnn_in['mlp_w1'], 'L0_gnn_mlp_b1': _L0_gnn_in['mlp_b1'], 'L0_gnn_mlp_w2': _L0_gnn_in['mlp_w2'], 'L0_gnn_mlp_b2': _L0_gnn_in['mlp_b2'], 'L0_gnn_eps': _L0_gnn_in['eps'], 'L0_gnn_out_w': _L0_gnn_in['out_w'], 'L0_gnn_out_b': _L0_gnn_in['out_b']}

def reference(x, src, dst, edge_attr_16, L0_gnn_enc_w, L0_gnn_enc_b, L0_gnn_edge_w, L0_gnn_edge_b, L0_gnn_mlp_w1, L0_gnn_mlp_b1, L0_gnn_mlp_w2, L0_gnn_mlp_b2, L0_gnn_eps, L0_gnn_out_w, L0_gnn_out_b):
    import jax
    import jax.numpy as jnp

    def _L0_gnn_ref(x, edge_index, edge_attr, enc_w, enc_b, edge_w, edge_b, mlp_w1, mlp_b1, mlp_w2, mlp_b2, eps, out_w, out_b):
        import jax, jax.numpy as jnp
        import numpy as np
        N, E = (6250, 100000)
        D, ED, L = (128, 16, 3)
        src = edge_index[0]
        dst = edge_index[1]
        n_nodes = x.shape[0]
        n_layers = eps.shape[0]
        h = x @ enc_w + enc_b
        h_list = [h]
        for l in range(n_layers):
            e = edge_attr @ edge_w[l] + edge_b[l]
            msg = jax.nn.relu(h_list[l][src] + e)
            agg = jax.ops.segment_sum(msg, dst, num_segments=n_nodes)
            z = (1.0 + eps[l]) * h_list[l] + agg
            z = jax.nn.relu(z @ mlp_w1[l] + mlp_b1[l]) @ mlp_w2[l] + mlp_b2[l]
            h_list.append(jax.nn.relu(z))
        hcat = jnp.concatenate(h_list, axis=1)
        return hcat @ out_w + out_b
    edge_index = jnp.stack([src, dst])
    h = jnp.maximum(_layernorm(x, axis=-1), 0.0)
    x = x + _L0_gnn_ref(h, edge_index, edge_attr_16, L0_gnn_enc_w, L0_gnn_enc_b, L0_gnn_edge_w, L0_gnn_edge_b, L0_gnn_mlp_w1, L0_gnn_mlp_b1, L0_gnn_mlp_w2, L0_gnn_mlp_b2, L0_gnn_eps, L0_gnn_out_w, L0_gnn_out_b)
    return x

_drawn_inputs = setup_inputs


def setup_inputs(seed=0):
    import zlib

    import numpy as np

    out = dict(_drawn_inputs(seed))
    spreads = {'L0_gnn_enc_b': (0.0, 0.1),
     'L0_gnn_edge_b': (0.0, 0.1),
     'L0_gnn_mlp_b1': (0.0, 0.1),
     'L0_gnn_mlp_b2': (0.0, 0.1),
     'L0_gnn_eps': (0.0, 0.1),
     'L0_gnn_out_b': (0.0, 0.1)}
    factors = {}
    for name, (base, spread) in spreads.items():
        noise = np.random.default_rng([zlib.crc32(name.encode()), seed]).standard_normal(out[name].shape)
        drawn = base * np.exp(spread * noise) if base else spread * noise
        out[name] = jnp.asarray(drawn.astype(out[name].dtype))
    for name, factor in factors.items():
        out[name] = (out[name] * factor).astype(out[name].dtype)
    return out
```

```python
import concourse.bass as bass
from concourse import mybir
from contextlib import ExitStack

P = 128
D = 128
KE = 16
WIN = 64
TG = 4
GC = 4
CB = 2
TC = TG * GC
GB = GC * CB
UNITS = (4, 3)
TB = sum(UNITS)


def gnn_kernel(nc, x_t, src_t, dst_t, dst_g, ea_t, enc_w, enc_b, edge_w, edge_b, w1, b1, w2, b2,
               eps, out_w, out_b, out):
    f32, i32 = mybir.dt.float32, mybir.dt.int32
    ALU, ACT, AX = mybir.AluOpType, mybir.ActivationFunctionType, mybir.AxisListType

    NT = x_t.shape[1] // D
    NP = NT * P
    NI = NT // TB
    NTE = src_t.shape[1]
    NB = NTE // (TC * CB)
    NCH = NB * CB
    NG = NCH * GC
    L = w1.shape[0]
    HC = w1.shape[2] // D
    UO = (0, UNITS[0])
    NL_G = NB * GB
    assert NT % TB == 0 and NTE % (TC * CB) == 0 and NCH <= P and HC == 2

    h_table = nc.dram_tensor("h_table", (NP, D), f32).ap()
    h_rows = h_table.rearrange("(t p) d -> p t d", p=P)
    spans_dram = nc.dram_tensor("spans", (2, NG), i32).ap()

    ctx = ExitStack()
    with ctx:
        def sb(name, shape, dt=f32):
            return ctx.enter_context(nc.sbuf_tensor(name, shape, dt))

        def sem(name):
            return ctx.enter_context(nc.semaphore(name))

        def sems(name, n):
            return [sem(f"{name}{i}") for i in range(n)]

        out_acc = sb("out_acc", [P, NT, D])
        agg_t = sb("agg_t", [P, NP + WIN])
        rows = sb("rows", [P, CB, TC, D])
        msg = [sb(f"msg{i}", [P, TG, D]) for i in range(2)]
        onehot = [sb(f"onehot{i}", [P, TG, WIN]) for i in range(2)]
        attr = [sb(f"attr{i}", [KE + 1, TC * P]) for i in range(CB)]
        idx = [sb(f"idx{i}", [P, TC], i32) for i in range(CB)]
        dst_rel = sb("dst_rel", [P, NTE])
        dst_far = sb("dst_far", [P, NTE])
        dst_i = sb("dst_i", [P, NTE], i32)
        dst_n = sb("dst_n", [NCH, GC, TG * P], i32)
        lo = sb("lo", [NCH, 2, GC])
        span = sb("span", [NCH, GC])
        spans_i = sb("spans_i", [NCH, 2, GC], i32)
        base_row = sb("base_row", [1, NG], i32)
        far_row = sb("far_row", [1, NG], i32)
        span_row = sb("span_row", [1, NG], i32)
        base_all = sb("base_all", [P, NG], i32)
        span_max = sb("span_max", [1, 1], i32)
        extra = sb("extra", [1, 1], i32)
        iota_i = sb("iota_i", [P, WIN], i32)
        iota = sb("iota", [P, WIN])
        ident = sb("ident", [P, P])
        encw = sb("encw", [P, D])
        encb = sb("encb", [P, 1])
        edgew = sb("edgew", [KE + 1, L, D])
        w1s = sb("w1s", [P, HC * D])
        w2s = sb("w2s", [P, HC, D])
        b1s = sb("b1s", [P, L * HC])
        b2s = sb("b2s", [P, L])
        outw = sb("outw", [P, L + 1, D])
        outb = sb("outb", [P, D])
        eps1 = sb("eps1", [P, L + 1])
        lneps = sb("lneps", [P, 1])
        stats = sb("stats", [P, NT, 6])
        mean = sb("mean", [P, NT])
        dif = sb("dif", [P, NT])
        var = sb("var", [P, NT])
        vs = sb("vs", [P, NT])
        std = sb("std", [P, NT])
        rstd = sb("rstd", [P, NT])
        nmr = sb("nmr", [P, NT])
        hn = [sb(f"hn{u}", [P, n, D]) for u, n in enumerate(UNITS)]
        hid = [sb(f"hid{u}", [P, HC, n * P]) for u, n in enumerate(UNITS)]
        h_t = [sb(f"h_t{u}", [P, n * P]) for u, n in enumerate(UNITS)]
        h_n = [sb(f"h_n{u}", [P, n, D]) for u, n in enumerate(UNITS)]

        bank = [ctx.enter_context(nc.psum_tensor(f"bank{i}", [P, 512], f32)) for i in range(8)]
        e_ps, agg_ps = bank[0:2], bank[2:4]
        z_ps = [bank[0:2], bank[2:4]]
        h_ps = bank[4:6]
        tr_ps, o_ps = bank[6], bank[7]

        s_par = sem("s_par")
        s_x = sems("s_x", 2)
        s_dst = sem("s_dst")
        s_span = sem("s_span")
        s_sp_out = sem("s_sp_out")
        s_sp_in = sem("s_sp_in")
        s_const = sem("s_const")
        s_cpy = sem("s_cpy")
        s_ready = sem("s_ready")
        s_var = sem("s_var")
        s_std = sem("s_std")
        s_norm = sem("s_norm")
        hn_ready = sems("hn_ready", 2)
        hn_turned = sems("hn_turned", 2)
        hn_moved = sems("hn_moved", 2)
        outb_added = sems("outb_added", 2)
        z_done = sems("z_done", 2)
        hid_ready = sems("hid_ready", 2)
        h_done = sems("h_done", 2)
        h_ready = sems("h_ready", 2)
        seeded = sems("seeded", 2)
        tr_done = sems("tr_done", 2)
        o_done = sems("o_done", 2)
        rows_ready = sems("rows_ready", 2)
        stored = sems("stored", 2)
        o_added = sems("o_added", 2)
        s_table = sem("s_table")
        s_w = sem("s_w")
        idx_in = sems("idx_in", CB)
        attr_in = sems("attr_in", CB)
        gathered = [sems(f"gathered{q}_", GC) for q in range(CB)]
        e_done = sem("e_done")
        hot = sem("hot")
        summed = sem("summed")
        msg_ready = sem("msg_ready")
        agg_done = sem("agg_done")
        added = sem("added")
        agg_all = sem("agg_all")
        f_next, f_idx, f_attr, f_rows, f_e, f_hot, f_sum, f_msg, f_agg, f_add, f_shift = (
            sem(n) for n in ("f_next", "f_idx", "f_attr", "f_rows", "f_e", "f_hot", "f_sum", "f_msg",
                             "f_agg", "f_add", "f_shift"))
        s_out = sem("s_out")
        s_passed = {eng.engine: sem(f"s_passed_{name}") for name, eng in (
            ("pool", nc.gpsimd), ("act", nc.scalar), ("pe", nc.tensor), ("dve", nc.vector))}

        N_PAR = 11
        block = ctx.enter_context(nc.Block())

        def take(eng, s, n):
            eng.wait_ge(s, n)
            eng.sem_clear(s)

        def wait_apart(eng, s, n):
            eng.wait_ge(s, n)
            eng.sem_inc(s_passed[eng.engine], 1)

        def far_passes(eng, one_pass):
            n = eng.value_load(extra[0:1, 0:1], min_val=0, max_val=NP // WIN + 1)
            with eng.If(n > 0):
                with eng.Fori(0, n):
                    one_pass()

        @block.sync
        def _(sp):
            sp.dma_start(dst_n[:, :, :], dst_g.rearrange("c (g e) -> c g e", g=GC)).then_inc(s_dst, 16)
            sp.dma_start(dst_i[:, :], dst_t).then_inc(s_dst, 16)
            for i, a, b in ((0, 0, NT // 2), (1, NT // 2, NT)):
                sp.dma_start(out_acc[:, a:b, :], x_t[:, a * D:b * D].rearrange("p (t d) -> p t d", d=D))\
                  .then_inc(s_x[i], 16)
            sp.dma_start(encw[:, :], enc_w).then_inc(s_par, 16)
            sp.dma_start(encb[:, :], enc_b).then_inc(s_par, 16)
            sp.dma_start(edgew[0:KE, :, :], edge_w.rearrange("l k n -> k l n")).then_inc(s_par, 16)
            sp.dma_start(edgew[KE:KE + 1, :, :], edge_b.rearrange("(a l) n -> a l n", a=1)).then_inc(s_par, 16)
            sp.dma_start(b1s[:, :], b1).then_inc(s_par, 16)
            sp.dma_start(b2s[:, :], b2).then_inc(s_par, 16)
            sp.dma_start(outw[:, :, :], out_w.rearrange("(l k) n -> k l n", k=D)).then_inc(s_par, 16)
            sp.dma_start(outb[:, :], out_b.partition_broadcast(P)).then_inc(s_par, 16)
            sp.dma_start(eps1[:, 0:L], eps.partition_broadcast(P)).then_inc(s_par, 16)
            sp.wait_ge(s_span, 1)
            for i in range(2):
                sp.dma_start(spans_dram[i, :].rearrange("(c g) -> c g", g=GC), spans_i[:, i, :])\
                  .then_inc(s_sp_out, 16)
            sp.wait_ge(s_sp_out, 32)
            sp.dma_start(base_row[:, :], spans_dram[0:1, :]).then_inc(s_sp_in, 16)
            sp.dma_start(far_row[:, :], spans_dram[0:1, :]).then_inc(s_sp_in, 16)
            sp.dma_start(span_row[:, :], spans_dram[1:2, :]).then_inc(s_sp_in, 16)
            sp.dma_start(base_all[:, :], spans_dram[0, :].partition_broadcast(P)).then_inc(s_sp_in, 16)

            def store_units(ph, last=False):
                with sp.Fori(0, NI) as i:
                    n = ph * NI + i
                    for u, w in enumerate(UNITS):
                        tile = i * TB + UO[u]
                        sp.wait_ge(rows_ready[u], n + 2)
                        sp.dma_start(h_rows[:, bass.ds(tile, w), :], h_n[u][:, :, :]).then_inc(stored[u], 16)
                        if last:
                            sp.wait_ge(o_added[u], n + 2)
                            sp.dma_start(out[:, bass.ds(tile * D, w * D)].rearrange("p (t d) -> p t d", d=D),
                                         out_acc[:, bass.ds(tile, w), :]).then_inc(s_out, 16)
                for u in range(2):
                    sp.wait_ge(stored[u], (ph * NI + NI) * 16 + 16)
                sp.sem_inc(s_table, 1)

            def far_pass():
                with sp.Fori(0, NG) as g:
                    take(sp, f_next, 1)
                    sp.dma_start(idx[0][:, 0:TG], src_t[:, bass.ds(g * TG, TG)]).then_inc(f_idx, 16)
                    sp.dma_start(attr[0][0:KE, 0:TG * P], ea_t[:, bass.ds(g * (TG * P), TG * P)])\
                      .then_inc(f_attr, 16)

            def layer(l, last):
                sp.dma_start(w1s[:, :], w1[bass.ds(l, 1), :, :].rearrange("a k n -> (a k) n")).then_inc(s_w, 16)
                sp.dma_start(w2s[:, :, :], w2[bass.ds(l, 1), :, :].rearrange("a (c p) n -> (a p) c n", p=D))\
                  .then_inc(s_w, 16)
                with sp.Fori(0, NB) as b:
                    n = l * NB + b
                    for q in range(CB):
                        c = b * CB + q
                        sp.wait_ge(summed, n * GB + (q + 1) * GC)
                        sp.dma_start(idx[q][:, :], src_t[:, bass.ds(c * TC, TC)]).then_inc(idx_in[q], 16)
                        sp.dma_start(attr[q][0:KE, :], ea_t[:, bass.ds(c * (TC * P), TC * P)])\
                          .then_inc(attr_in[q], 16)
                far_passes(sp, far_pass)
                store_units(l + 1, last)

            sp.wait_ge(s_const, 4)
            store_units(0)
            sp.wait_ge(s_ready, 1)
            with sp.Fori(0, L - 1) as l:
                layer(l, False)
            layer(L - 1, True)
            sp.wait_ge(s_out, 16 * 2 * NI)

        @block.gpsimd
        def _(g):
            for q in range(CB):
                g.memset(attr[q][:, :], 1.0).then_inc(s_const, 1)
            g.memset(ident[:, :], 0.0).then_inc(s_const, 1)
            g.iota(iota_i[:, :], pattern=[[1, WIN]], base=0, channel_multiplier=0).then_inc(s_const, 1)
            g.wait_ge(s_const, 4)
            g.affine_select(out=ident[:, :], in_=ident[:, :], compare_op=ALU.not_equal, fill=1.0, base=0,
                            pattern=[[-1, P]], channel_multiplier=1).then_inc(s_const, 1)
            g.memset(agg_t[:, NP:NP + WIN], 0.0).then_inc(s_const, 1)
            g.memset(eps1[:, L:L + 1], 0.0).then_inc(s_const, 1)
            g.memset(lneps[:, :], 1e-5).then_inc(s_const, 1)
            for u in range(2):
                g.sem_inc(stored[u], 16)
            g.wait_ge(s_par, 16 * (N_PAR - 2))
            with g.Fori(0, NI) as i:
                for u, w in enumerate(UNITS):
                    acc = out_acc[:, bass.ds(i * TB + UO[u], w), :]
                    g.wait_ge(hn_ready[u], i + 1)
                    g.tensor_tensor(acc, acc, outb[:, :].unsqueeze(1).broadcast_to([P, w, D]), ALU.add)\
                     .then_inc(outb_added[u], 1)
            g.wait_ge(s_ready, 1)

            def gather(dst, index):
                return g.indirect_dma_start(dst, None, h_table, bass.IndirectOffsetOnAxis(ap=index, axis=0))

            def far_pass():
                with g.Fori(0, NG):
                    take(g, f_idx, 16)
                    for j in range(TG):
                        gather(rows[:, 0, j, :], idx[0][:, j:j + 1]).then_inc(f_rows, 16)

            with g.Fori(0, L) as l:
                wait_apart(g, s_table, l + 1)
                with g.Fori(0, NB) as b:
                    n = l * NB + b
                    for q in range(CB):
                        g.wait_ge(idx_in[q], n * 16 + 16)
                        wait_apart(g, msg_ready, n * GB + (q + 1) * GC)
                        for k in range(GC):
                            for j in range(TG):
                                t = k * TG + j
                                gather(rows[:, q, t, :], idx[q][:, t:t + 1]).then_inc(gathered[q][k], 16)
                far_passes(g, far_pass)

        @block.scalar
        def _(act):
            act.sem_inc(msg_ready, GB)
            for u in range(2):
                act.sem_inc(hid_ready[u], HC)
                act.sem_inc(h_ready[u], 1)
            act.wait_ge(s_const, 8)
            act.wait_ge(s_par, 16 * (N_PAR - 2))
            act.wait_ge(s_var, 1)
            nc.scalar.activation(std[:, :], var[:, :], ACT.Sqrt, bias=lneps[:, 0:1]).then_inc(s_std, 1)

            def take_h(u, n, func, bias):
                act.wait_ge(h_done[u], n + 1)
                act.wait_ge(o_done[u], n + 1)
                wait_apart(act, seeded[u], n + 1)
                nc.scalar.activation(h_t[u][:, :], h_ps[u][:, 0:UNITS[u] * P], func, bias=bias)\
                  .then_inc(h_ready[u], 1)

            act.wait_ge(s_norm, 1)
            with act.Fori(0, NI) as i:
                for u, w in enumerate(UNITS):
                    for j in range(w):
                        t = i * TB + (UO[u] + j)
                        last = nc.scalar.activation(
                            hn[u][:, j:j + 1, :], out_acc[:, bass.ds(t, 1), :], ACT.Relu,
                            bias=nmr[:, bass.ds(t, 1)], scale=rstd[:, bass.ds(t, 1)])
                    last.then_inc(hn_ready[u], 1)
                for u in range(2):
                    take_h(u, i, ACT.Identity, encb[:, 0:1])
            act.wait_ge(s_ready, 1)

            def far_pass():
                with act.Fori(0, NG):
                    take(act, f_sum, 1)
                    nc.scalar.activation(msg[0][:, :, :], rows[:, 0, 0:TG, :], ACT.Relu).then_inc(f_msg, 1)

            with act.Fori(0, L) as l:
                with act.Fori(0, NB) as b:
                    n = l * NB + b
                    for k in range(GB):
                        q, t = k // GC, k % GC * TG
                        act.wait_ge(summed, n * GB + (k + 1 + GB))
                        act.wait_ge(agg_done, n * GB + (k + 1))
                        nc.scalar.activation(msg[k % 2][:, :, :], rows[:, q, t:t + TG, :], ACT.Relu)\
                          .then_inc(msg_ready, 1)
                far_passes(act, far_pass)
                with act.Fori(0, NI) as i:
                    n = l * NI + i
                    for u, w in enumerate(UNITS):
                        for c in range(HC):
                            wait_apart(act, z_done[u], n * HC + (c + 1))
                            nc.scalar.activation(hid[u][:, c, :], z_ps[u][c][:, 0:w * P], ACT.Relu,
                                                 bias=b1s[:, bass.ds(l * HC + c, 1)]).then_inc(hid_ready[u], 1)
                    for u in range(2):
                        take_h(u, n + NI, ACT.Relu, b2s[:, bass.ds(l, 1)])

        @block.tensor
        def _(pe):
            pe.sem_inc(agg_done, 2)
            for u in range(2):
                pe.sem_inc(o_done[u], 1)
            pe.wait_ge(s_const, 8)
            pe.wait_ge(s_par, 16 * (N_PAR - 2))

            def publish(u, n, ph):
                w = UNITS[u]
                pe.wait_ge(h_ready[u], n + 2)
                pe.wait_ge(rows_ready[1 - u], n + 1 if u == 0 else n + 2)
                for j in range(w):
                    last = nc.tensor.transpose(tr_ps[:, j * P:(j + 1) * P], h_t[u][:, j * P:(j + 1) * P], ident[:, :])
                last.then_inc(tr_done[u], 1)
                pe.wait_ge(o_added[1 - u], n + 1 if u == 0 else n + 2)
                for j in range(w):
                    last = nc.tensor.matmul(o_ps[:, j * P:(j + 1) * P], h_t[u][:, j * P:(j + 1) * P],
                                            outw[:, bass.ds(ph, 1), :].rearrange("p a n -> p (a n)"),
                                            start=True, stop=True)
                last.then_inc(o_done[u], 1)

            with pe.Fori(0, NI) as i:
                for u, w in enumerate(UNITS):
                    pe.wait_ge(hn_ready[u], i + 1)
                    pe.wait_ge(hn_moved[u], i + 1)
                    for j in range(w):
                        last = nc.tensor.transpose(z_ps[u][0][:, j * P:(j + 1) * P], hn[u][:, j, :], ident[:, :])
                    last.then_inc(hn_turned[u], 1)
                for u, w in enumerate(UNITS):
                    pe.wait_ge(hn_moved[u], i + 2)
                    pe.wait_ge(h_ready[u], i + 1)
                    nc.tensor.matmul(h_ps[u][:, 0:w * P], encw[:, :], hid[u][:, 0, :], start=True, stop=True)\
                      .then_inc(h_done[u], 1)
                for u in range(2):
                    publish(u, i, 0)
            pe.wait_ge(s_ready, 1)

            def edge_terms(dst, cols, l):
                for j in range(TG):
                    last = nc.tensor.matmul(dst[:, j * D:(j + 1) * D], cols[:, j * P:(j + 1) * P],
                                            edgew[:, bass.ds(l, 1), :].rearrange("p a n -> p (a n)"),
                                            start=True, stop=True)
                return last

            def window_sums(dst, m, hot_m):
                for j in range(TG):
                    last = nc.tensor.matmul(dst[:, 0:WIN], m[:, j, :], hot_m[:, j, :],
                                            start=(j == 0), stop=(j == TG - 1))
                return last

            with pe.Fori(0, L) as l:

                def far_pass():
                    with pe.Fori(0, NG):
                        take(pe, f_attr, 16)
                        edge_terms(e_ps[0], attr[0], l).then_inc(f_e, 1)
                        take(pe, f_hot, 1)
                        take(pe, f_msg, 1)
                        window_sums(agg_ps[0], msg[0], onehot[0]).then_inc(f_agg, 1)

                with pe.Fori(0, NB) as b:
                    n = l * NB + b

                    def sums(k):
                        pe.wait_ge(msg_ready, n * GB + (k + 1 + GB))
                        pe.wait_ge(hot, n * GB + (k + 1))
                        pe.wait_ge(added, n * GB + (k + 1))
                        window_sums(agg_ps[k % 2], msg[k % 2], onehot[k % 2]).then_inc(agg_done, 1)

                    for k in range(GB):
                        q, t = k // GC, k % GC * TG
                        if k % GC == 0:
                            wait_apart(pe, attr_in[q], n * 16 + 16)
                        wait_apart(pe, summed, n * GB + (k + GB - 1))
                        edge_terms(e_ps[k % 2], attr[q][:, t * P:(t + TG) * P], l).then_inc(e_done, 1)
                        if k:
                            sums(k - 1)
                    sums(GB - 1)
                far_passes(pe, far_pass)
                pe.wait_ge(s_w, l * 32 + 32)
                wait_apart(pe, agg_all, l + 1)
                with pe.Fori(0, NI) as i:
                    n = l * NI + i
                    for u, w in enumerate(UNITS):
                        cols = agg_t[:, bass.ds((i * TB + UO[u]) * P, w * P)]
                        for c in range(HC):
                            pe.wait_ge(hid_ready[u], n * HC + (c + 1))
                            nc.tensor.matmul(z_ps[u][c][:, 0:w * P], w1s[:, c * D:(c + 1) * D], cols,
                                             start=True, stop=True).then_inc(z_done[u], 1)
                    for u, w in enumerate(UNITS):
                        pe.wait_ge(h_ready[u], n + (NI + 1))
                        for c in range(HC):
                            pe.wait_ge(hid_ready[u], n * HC + (c + 1 + HC))
                            last = nc.tensor.matmul(h_ps[u][:, 0:w * P], w2s[:, c, :], hid[u][:, c, :],
                                                    start=(c == 0), stop=(c == HC - 1))
                        last.then_inc(h_done[u], 1)
                    for u in range(2):
                        publish(u, n + NI, l + 1)

        @block.vector
        def _(dve):
            dve.sem_inc(summed, GB)
            dve.sem_inc(added, 2)
            for u in range(2):
                dve.sem_inc(hn_moved[u], 1)
                dve.sem_inc(seeded[u], 1)
                dve.sem_inc(rows_ready[u], 1)
                dve.sem_inc(o_added[u], 1)
            v = nc.vector
            step = [0]

            def own(ins):
                step[0] += 1
                ins.then_inc(s_cpy, 1)
                dve.wait_ge(s_cpy, step[0])

            dve.wait_ge(s_dst, 32)
            own(v.tensor_reduce(lo[:, 0, :], dst_n[:, :, :], AX.X, ALU.min))
            own(v.tensor_reduce(lo[:, 1, :], dst_n[:, :, :], AX.X, ALU.max))
            own(v.tensor_tensor(span[:, :], lo[:, 1, :], lo[:, 0, :], ALU.subtract))
            own(v.tensor_copy(spans_i[:, 0, :], lo[:, 0, :]))
            v.tensor_copy(spans_i[:, 1, :], span[:, :]).then_inc(s_span, 1)
            for half in range(2):
                dve.wait_ge(s_x[half], 16)
                with dve.Fori(half * NI // 2, (half + 1) * NI // 2) as i:
                    for j in range(TB):
                        t = i * TB + j
                        last = v.bn_stats(stats[:, bass.ds(t, 1), :].rearrange("p a s -> p (a s)"),
                                          out_acc[:, bass.ds(t, 1), :].rearrange("p a d -> p (a d)"))
                    last.then_inc(s_cpy, 1)
            step[0] += NI
            dve.wait_ge(s_cpy, step[0])
            own(v.tensor_tensor(dif[:, :], stats[:, :, 1], stats[:, :, 4], ALU.subtract))
            own(v.tensor_tensor(dif[:, :], dif[:, :], dif[:, :], ALU.mult))
            own(v.tensor_tensor(vs[:, :], stats[:, :, 2], stats[:, :, 5], ALU.add))
            own(v.tensor_scalar(vs[:, :], vs[:, :], 1.0 / D, None, ALU.mult))
            v.scalar_tensor_tensor(out=var[:, :], in0=dif[:, :], scalar=0.25, in1=vs[:, :], op0=ALU.mult,
                                   op1=ALU.add).then_inc(s_var, 1)
            own(v.tensor_tensor(mean[:, :], stats[:, :, 1], stats[:, :, 4], ALU.add))
            dve.wait_ge(s_std, 1)
            own(v.reciprocal(rstd[:, :], std[:, :]))
            v.scalar_tensor_tensor(out=nmr[:, :], in0=mean[:, :], scalar=-0.5, in1=rstd[:, :], op0=ALU.mult,
                                   op1=ALU.mult).then_inc(s_norm, 1)
            dve.wait_ge(s_const, 8)
            dve.wait_ge(s_par, 16 * (N_PAR - 2))
            own(v.tensor_scalar(eps1[:, :], eps1[:, :], 1.0, None, ALU.add))
            own(v.tensor_copy(iota[:, :], iota_i[:, :]))
            dve.wait_ge(s_sp_in, 64)
            own(v.tensor_tensor(dst_rel[:, :].rearrange("p (g t) -> p g t", t=TG),
                                dst_i[:, :].rearrange("p (g t) -> p g t", t=TG),
                                base_all[:, :].unsqueeze(2).broadcast_to([P, NG, TG]), ALU.subtract))
            own(v.tensor_copy(dst_far[:, :], dst_rel[:, :]))
            own(v.tensor_reduce(span_max[:, :], span_row[:, :], AX.X, ALU.max))
            own(v.tensor_single_scalar(extra[:, :], span_max[:, :], WIN.bit_length() - 1, ALU.arith_shift_right))
            dve.sem_inc(s_ready, 1)

            def publish(u, i, n, ph, first=False):
                w = UNITS[u]
                tile = i * TB + UO[u]
                dve.wait_ge(h_ready[u], n + 2)
                v.tensor_scalar(agg_t[:, bass.ds(tile * P, w * P)], h_t[u][:, :], eps1[:, bass.ds(ph, 1)], None,
                                ALU.mult).then_inc(seeded[u], 1)
                dve.wait_ge(tr_done[u], n + 1)
                dve.wait_ge(stored[u], n * 16 + 16)
                v.tensor_copy(h_n[u][:, :, :], tr_ps[:, 0:w * P].rearrange("p (t d) -> p t d", d=D))\
                 .then_inc(rows_ready[u], 1)
                dve.wait_ge(o_done[u], n + 2)
                if first:
                    dve.wait_ge(outb_added[u], n + 1)
                acc = out_acc[:, bass.ds(tile, w), :]
                v.tensor_tensor(acc, o_ps[:, 0:w * P].rearrange("p (t d) -> p t d", d=D), acc, ALU.add)\
                 .then_inc(o_added[u], 1)

            with dve.Fori(0, NI) as i:
                for u, w in enumerate(UNITS):
                    dve.wait_ge(hn_turned[u], i + 1)
                    v.tensor_copy(hid[u][:, 0, :], z_ps[u][0][:, 0:w * P]).then_inc(hn_moved[u], 1)
                for u in range(2):
                    publish(u, i, i, 0, first=True)

            def one_hot(dst, rel, g):
                return v.tensor_tensor(dst[:, :, :], iota[:, :].unsqueeze(1).broadcast_to([P, TG, WIN]),
                                       rel[:, bass.ds(g * TG, TG)].unsqueeze(2).broadcast_to([P, TG, WIN]),
                                       ALU.is_equal)

            def load_base(table, g):
                return dve.value_load(table[0:1, bass.ds(g, 1)], min_val=0, max_val=NP)

            def add_window(base, ps):
                cols = agg_t[:, bass.ds(base, WIN)]
                return v.tensor_tensor(cols, ps[:, 0:WIN], cols, ALU.add)

            rows_seen = dve.alloc_register("rows_seen")
            dve.reg_mov(rows_seen, 0)

            def far_pass():
                v.tensor_scalar(dst_far[:, :], dst_far[:, :], float(WIN), None, ALU.subtract).then_inc(f_shift, 1)
                v.tensor_scalar(far_row[:, :], far_row[:, :], float(WIN), float(NP), ALU.add, ALU.min)\
                 .then_inc(f_shift, 1)
                take(dve, f_shift, 2)
                with dve.Fori(0, NG) as g:
                    dve.sem_inc(f_next, 1)
                    one_hot(onehot[0], dst_far, g).then_inc(f_hot, 1)
                    take(dve, f_e, 1)
                    dve.reg_add(rows_seen, rows_seen, 16 * TG)
                    dve.wait_ge(f_rows, dve.snap(rows_seen, min_val=16 * TG))
                    v.tensor_tensor(rows[:, 0, 0:TG, :], e_ps[0][:, :].rearrange("p (t d) -> p t d", d=D),
                                    rows[:, 0, 0:TG, :], ALU.add).then_inc(f_sum, 1)
                    base = load_base(far_row, g)
                    take(dve, f_agg, 1)
                    add_window(base, agg_ps[0]).then_inc(f_add, 1)
                    take(dve, f_add, 1)

            with dve.Fori(0, L) as l:
                for u in range(2):
                    wait_apart(dve, seeded[u], l * NI + (NI + 1))
                with dve.Fori(0, NB) as b:
                    n = l * NB + b

                    def accumulate(k):
                        base = load_base(base_row, b * GB + k)
                        dve.wait_ge(agg_done, n * GB + (k + 3))
                        dve.wait_ge(added, n * GB + (k + 2))
                        add_window(base, agg_ps[k % 2]).then_inc(added, 1)

                    for k in range(GB):
                        q, t = k // GC, k % GC * TG
                        dve.wait_ge(agg_done, n * GB + (k + 1))
                        one_hot(onehot[k % 2], dst_rel, b * GB + k).then_inc(hot, 1)
                        dve.wait_ge(e_done, n * GB + (k + 1))
                        dve.wait_ge(gathered[q][k % GC], n * (16 * TG) + 16 * TG)
                        part = rows[:, q, t:t + TG, :]
                        v.tensor_tensor(part, e_ps[k % 2][:, :].rearrange("p (t d) -> p t d", d=D), part, ALU.add)\
                         .then_inc(summed, 1)
                        if k:
                            accumulate(k - 1)
                    accumulate(GB - 1)
                wait_apart(dve, added, l * NL_G + (NL_G + 2))
                far_passes(dve, far_pass)
                dve.sem_inc(agg_all, 1)
                v.tensor_copy(dst_far[:, :], dst_rel[:, :]).then_inc(f_shift, 1)
                v.tensor_copy(far_row[:, :], base_row[:, :]).then_inc(f_shift, 1)
                take(dve, f_shift, 2)
                with dve.Fori(0, NI) as i:
                    for u in range(2):
                        publish(u, i, l * NI + i + NI, l + 1)


def _layout(a, tiles_up_to):
    import numpy as np

    n = a.shape[0]
    rows = -(-n // (P * tiles_up_to)) * P * tiles_up_to
    padded = np.zeros((rows, *a.shape[1:]), a.dtype)
    padded[:n] = a
    return np.ascontiguousarray(np.moveaxis(padded.reshape(-1, P, *a.shape[1:]), 0, 1)).reshape(P, -1)


def kernel(x, src, dst, edge_attr_16, L0_gnn_enc_w, L0_gnn_enc_b, L0_gnn_edge_w, L0_gnn_edge_b, L0_gnn_mlp_w1,
           L0_gnn_mlp_b1, L0_gnn_mlp_w2, L0_gnn_mlp_b2, L0_gnn_eps, L0_gnn_out_w, L0_gnn_out_b):
    import numpy as np
    import concourse.bacc as bacc
    from concourse.bass_utils import run_bass_kernel_spmd

    x, src, dst, ea = (np.asarray(a) for a in (x, src, dst, edge_attr_16))
    n, e = x.shape[0], src.shape[0]
    ep = -(-e // (P * TC * CB)) * P * TC * CB
    dst_p = np.full(ep, n, dst.dtype)
    dst_p[:e] = dst
    ea_p = np.zeros((KE, ep), ea.dtype)
    ea_p[:, :e] = ea.T
    arrays = {
        "x_t": _layout(x, TB),
        "src_t": _layout(src, TC * CB),
        "dst_t": _layout(dst_p, TC * CB),
        "dst_g": dst_p.reshape(-1, P * TC),
        "ea_t": ea_p,
        "enc_w": np.asarray(L0_gnn_enc_w),
        "enc_b": np.asarray(L0_gnn_enc_b).reshape(D, 1),
        "edge_w": np.asarray(L0_gnn_edge_w),
        "edge_b": np.asarray(L0_gnn_edge_b),
        "w1": np.asarray(L0_gnn_mlp_w1),
        "b1": np.ascontiguousarray(np.asarray(L0_gnn_mlp_b1).reshape(-1, D).T),
        "w2": np.asarray(L0_gnn_mlp_w2),
        "b2": np.ascontiguousarray(np.asarray(L0_gnn_mlp_b2).T),
        "eps": np.asarray(L0_gnn_eps),
        "out_w": np.asarray(L0_gnn_out_w),
        "out_b": np.asarray(L0_gnn_out_b),
    }
    nc = bacc.Bacc("TRN2", target_bir_lowering=False, num_devices=1)
    args = {k: nc.dram_tensor(k, a.shape, mybir.dt.from_np(a.dtype), kind="ExternalInput").ap()
            for k, a in arrays.items()}
    args["out"] = nc.dram_tensor("out", arrays["x_t"].shape, mybir.dt.float32, kind="ExternalOutput").ap()
    gnn_kernel(nc, **args)
    r = run_bass_kernel_spmd(nc, [arrays], core_ids=[0])
    got = r.results[0]["out"].reshape(P, -1, D)
    return np.moveaxis(got, 1, 0).reshape(-1, D)[:n]
```

```python
import concourse.bass as bass
from concourse import mybir
from contextlib import ExitStack

P = 128
D = 128
KE = 16
WIN = 64
TG = 4
GC = 2
CB = 4
TC = TG * GC
GB = GC * CB
GR = 4
UNITS = (4, 3)
TB = sum(UNITS)


def gnn_kernel(nc, x_t, src_t, dst_t, dst_g, ea_t, enc_w, enc_b, edge_w, edge_b, w1, b1, w2, b2,
               eps, out_w, out_b, out):
    f32, i32 = mybir.dt.float32, mybir.dt.int32
    ALU, ACT, AX = mybir.AluOpType, mybir.ActivationFunctionType, mybir.AxisListType

    NT = x_t.shape[1] // D
    NP = NT * P
    NI = NT // TB
    NTE = src_t.shape[1]
    NB = NTE // (TC * CB)
    NCH = NB * CB
    NG = NCH * GC
    L = w1.shape[0]
    HC = w1.shape[2] // D
    UO = (0, UNITS[0])
    assert NT % TB == 0 and NTE % (TC * CB) == 0 and NG <= P * GR and HC == 2 and NI % 2 == 0

    h_table = nc.dram_tensor("h_table", (2 * NP, D), f32).ap()
    src_l = nc.dram_tensor("src_l", (L, P, NTE), i32).ap()
    h_rows = h_table.rearrange("(t p) d -> p t d", p=P)
    spans_dram = nc.dram_tensor("spans", (2, NG), i32).ap()

    ctx = ExitStack()
    with ctx:
        def sb(name, shape, dt=f32):
            return ctx.enter_context(nc.sbuf_tensor(name, shape, dt))

        def sem(name):
            return ctx.enter_context(nc.semaphore(name))

        def sems(name, n):
            return [sem(f"{name}{i}") for i in range(n)]

        out_acc = sb("out_acc", [P, NT, D])
        agg_t = sb("agg_t", [P, NP + WIN])
        rows = sb("rows", [P, CB, TC, D])
        msg = [sb(f"msg{i}", [P, TG, D]) for i in range(2)]
        onehot = [sb(f"onehot{i}", [P, TG, WIN]) for i in range(2)]
        attr = [sb(f"attr{i}", [KE + 1, TC * P]) for i in range(CB)]
        idx = [sb(f"idx{i}", [P, TC], i32) for i in range(CB)]
        dst_rel = sb("dst_rel", [P, NTE])
        dst_far = sb("dst_far", [P, NTE])
        dst_i = sb("dst_i", [P, NTE], i32)
        dst_n = sb("dst_n", [NG // GR, GR, TG * P], i32)
        lo = sb("lo", [NG // GR, 2, GR])
        span = sb("span", [NG // GR, GR])
        spans_i = sb("spans_i", [NG // GR, 2, GR], i32)
        base_row = sb("base_row", [1, NG], i32)
        far_row = sb("far_row", [1, NG], i32)
        span_row = sb("span_row", [1, NG], i32)
        base_all = sb("base_all", [P, NG], i32)
        span_max = sb("span_max", [1, 1], i32)
        src_i = dst_far[:, :].bitcast(i32)
        later_lo = [sb(f"later_lo{i}", [1, NB]) for i in range(2)]
        ends_i = sb("ends_i", [1, NI], i32)
        ends = sb("ends", [1, NI])
        below = dst_n[0:1, :, :].rearrange("a g e -> a (g e)").bitcast(f32)[:, 0:NB * NI]\
            .rearrange("a (b i) -> a b i", i=NI)
        no_far = sb("no_far", [1, 1])
        stop_f = sb("stop_f", [1, NB])
        node_stop = sb("node_stop", [1, NB + 1], i32)
        extra = sb("extra", [1, 1], i32)
        iota_i = sb("iota_i", [P, WIN], i32)
        iota = sb("iota", [P, WIN])
        ident = sb("ident", [P, P])
        encw = sb("encw", [P, D])
        encb = sb("encb", [P, 1])
        edgew = sb("edgew", [KE + 1, L, D])
        w1s = sb("w1s", [P, HC * D])
        w2s = sb("w2s", [P, HC, D])
        b1s = sb("b1s", [P, L * HC])
        b2s = sb("b2s", [P, L])
        outw = sb("outw", [P, L + 1, D])
        outb = sb("outb", [P, D])
        eps1 = sb("eps1", [P, L + 1])
        lneps = sb("lneps", [P, 1])
        stats = sb("stats", [P, NT, 6])
        mean = sb("mean", [P, NT])
        dif = sb("dif", [P, NT])
        var = sb("var", [P, NT])
        vs = sb("vs", [P, NT])
        std = sb("std", [P, NT])
        rstd = sb("rstd", [P, NT])
        nmr = sb("nmr", [P, NT])
        hn = [sb(f"hn{u}", [P, n, D]) for u, n in enumerate(UNITS)]
        hid = [sb(f"hid{u}", [P, HC, n * P]) for u, n in enumerate(UNITS)]
        h_t = [sb(f"h_t{u}", [P, n * P]) for u, n in enumerate(UNITS)]
        h_n = [sb(f"h_n{u}", [P, n, D]) for u, n in enumerate(UNITS)]

        bank = [ctx.enter_context(nc.psum_tensor(f"bank{i}", [P, 512], f32)) for i in range(8)]
        e_ps, agg_ps = bank[0:2], bank[2:4]
        z_ps, h_ps, o_ps = bank[4:6], bank[6], bank[7]
        tr_ps = z_ps[0]
        src_up = rows[:, :, :, :].rearrange("p q t d -> p (q t d)").bitcast(i32)[:, 0:NTE]

        s_par = sem("s_par")
        s_x = sems("s_x", 2)
        s_dst = sem("s_dst")
        s_dst_t = sem("s_dst_t")
        s_span = sem("s_span")
        s_sp_out = sem("s_sp_out")
        s_sp_in = sem("s_sp_in")
        s_const = sem("s_const")
        s_cpy = sem("s_cpy")
        s_ready = sem("s_ready")
        s_src = sem("s_src")
        s_src_up = sem("s_src_up")
        s_fill = sem("s_fill")
        s_src_out = sem("s_src_out")
        s_var = sem("s_var")
        s_std = sem("s_std")
        s_stats = sem("s_stats")
        s_norm = sem("s_norm")
        hn_ready = sems("hn_ready", 2)
        hn_turned = sems("hn_turned", 2)
        hn_moved = sems("hn_moved", 2)
        outb_added = sems("outb_added", 2)
        z_done = sems("z_done", 2)
        hid_ready = sems("hid_ready", 2)
        h_done = sems("h_done", 2)
        h_ready = sems("h_ready", 2)
        seeded = sems("seeded", 2)
        tr_done = sems("tr_done", 2)
        o_done = sems("o_done", 2)
        rows_ready = sems("rows_ready", 2)
        stored = sems("stored", 2)
        o_added = sems("o_added", 2)
        s_w = sem("s_w")
        idx_in = sems("idx_in", CB)
        attr_in = sems("attr_in", CB)
        gathered = [sems(f"gathered{q}_", GC) for q in range(CB)]
        e_done = sem("e_done")
        hot = sem("hot")
        summed = sem("summed")
        msg_ready = sem("msg_ready")
        agg_done = sem("agg_done")
        added = sem("added")
        agg_all = sem("agg_all")
        f_next, f_idx, f_attr, f_rows, f_got, f_e, f_hot, f_sum, f_msg, f_agg, f_add, f_shift = (
            sem(n) for n in ("f_next", "f_idx", "f_attr", "f_rows", "f_got", "f_e", "f_hot", "f_sum", "f_msg",
                             "f_agg", "f_add", "f_shift"))
        s_out = sem("s_out")
        s_passed = {eng.engine: sem(f"s_passed_{name}") for name, eng in (
            ("pool", nc.gpsimd), ("act", nc.scalar), ("pe", nc.tensor), ("dve", nc.vector))}

        N_PAR = 9
        block = ctx.enter_context(nc.Block())

        def take(eng, s, n):
            eng.wait_ge(s, n)
            eng.sem_clear(s)

        def wait_apart(eng, s, n):
            eng.wait_ge(s, n)
            eng.sem_inc(s_passed[eng.engine], 1)

        def far_passes(eng, one_pass):
            n = eng.value_load(extra[0:1, 0:1], min_val=0, max_val=NP // WIN + 1)
            with eng.If(n > 0):
                with eng.Fori(0, n):
                    one_pass()

        def nodes_before(eng, b, node_body):
            first = eng.value_load(node_stop[0:1, bass.ds(b, 1)], min_val=0, max_val=NI)
            stop = eng.value_load(node_stop[0:1, bass.ds(b + 1, 1)], min_val=0, max_val=NI)
            with eng.If(first < stop):
                with eng.Fori(first, stop) as i:
                    node_body(i)

        def nodes_left(eng, node_body):
            first = eng.value_load(node_stop[0:1, NB:NB + 1], min_val=0, max_val=NI)
            with eng.If(first < NI):
                with eng.Fori(first, NI) as i:
                    node_body(i)

        @block.sync
        def _(sp):
            sp.dma_start(dst_n[:, :, :], dst_g.rearrange("c (g e) -> c g e", g=GR)).then_inc(s_dst, 16)
            for i, a, b in ((0, 0, NT // 2), (1, NT // 2, NT)):
                sp.dma_start(out_acc[:, a:b, :], x_t[:, a * D:b * D].rearrange("p (t d) -> p t d", d=D))\
                  .then_inc(s_x[i], 16)
            sp.dma_start(dst_i[:, :], dst_t).then_inc(s_dst_t, 16)
            sp.dma_start(src_i, src_t).then_inc(s_src, 16)
            for l in range(0, L, 2):
                sp.dma_start(src_l[l, :, :], src_t).then_inc(s_src_out, 16)
            for i, a, b in ((0, 0, NT // 2), (1, NT // 2, NT)):
                sp.wait_ge(s_x[i], 16)
                sp.dma_start(h_rows[:, NT + a:NT + b, :], out_acc[:, a:b, :]).then_inc(s_fill, 16)
            sp.dma_start(encw[:, :], enc_w).then_inc(s_par, 16)
            sp.dma_start(encb[:, :], enc_b).then_inc(s_par, 16)
            sp.dma_start(edgew[0:KE, :, :], edge_w.rearrange("l k n -> k l n")).then_inc(s_par, 16)
            sp.dma_start(edgew[KE:KE + 1, :, :], edge_b.rearrange("(a l) n -> a l n", a=1)).then_inc(s_par, 16)
            sp.dma_start(b1s[:, :], b1).then_inc(s_par, 16)
            sp.dma_start(b2s[:, :], b2).then_inc(s_par, 16)
            sp.dma_start(outw[:, :, :], out_w.rearrange("(l k) n -> k l n", k=D)).then_inc(s_par, 16)
            sp.dma_start(outb[:, :], out_b.partition_broadcast(P)).then_inc(s_par, 16)
            sp.dma_start(eps1[:, 0:L], eps.partition_broadcast(P)).then_inc(s_par, 16)
            sp.wait_ge(s_span, 1)
            for i in range(2):
                sp.dma_start(spans_dram[i, :].rearrange("(c g) -> c g", g=GR), spans_i[:, i, :])\
                  .then_inc(s_sp_out, 16)
            sp.wait_ge(s_sp_out, 32)
            sp.dma_start(base_row[:, :], spans_dram[0:1, :]).then_inc(s_sp_in, 16)
            sp.dma_start(far_row[:, :], spans_dram[0:1, :]).then_inc(s_sp_in, 16)
            sp.dma_start(span_row[:, :], spans_dram[1:2, :]).then_inc(s_sp_in, 16)
            sp.dma_start(base_all[:, :], spans_dram[0, :].partition_broadcast(P)).then_inc(s_sp_in, 16)

            sp.wait_ge(s_src_up, 1)
            for l in range(1, L, 2):
                sp.dma_start(src_l[l, :, :], src_up).then_inc(s_src_out, 16)

            sp.wait_ge(s_const, CB)
            sp.wait_ge(s_src_out, 16 * L)
            sp.wait_ge(s_ready, 1)
            with sp.Fori(0, L) as l:
                layer_src = src_l[bass.ds(l, 1), :, :].rearrange("a p t -> (a p) t")

                def far_pass():
                    with sp.Fori(0, NG) as g:
                        take(sp, f_next, 1)
                        sp.dma_start(idx[0][:, 0:TG], layer_src[:, bass.ds(g * TG, TG)]).then_inc(f_idx, 16)
                        sp.dma_start(attr[0][0:KE, 0:TG * P], ea_t[:, bass.ds(g * (TG * P), TG * P)])\
                          .then_inc(f_attr, 16)

                for u in range(2):
                    sp.wait_ge(h_ready[u], l * NI + (NI + 1))
                sp.dma_start(w1s[:, :], w1[bass.ds(l, 1), :, :].rearrange("a k n -> (a k) n")).then_inc(s_w, 16)
                sp.dma_start(w2s[:, :, :], w2[bass.ds(l, 1), :, :].rearrange("a (c p) n -> (a p) c n", p=D))\
                  .then_inc(s_w, 16)
                with sp.Fori(0, NB) as b:
                    n = l * NB + b
                    for q in range(CB):
                        c = b * CB + q
                        sp.wait_ge(summed, n * GB + (q + 1) * GC)
                        sp.dma_start(idx[q][:, :], layer_src[:, bass.ds(c * TC, TC)]).then_inc(idx_in[q], 16)
                        sp.dma_start(attr[q][0:KE, :], ea_t[:, bass.ds(c * (TC * P), TC * P)])\
                          .then_inc(attr_in[q], 16)
                far_passes(sp, far_pass)
            with sp.Fori(0, NI) as i:
                for u, w in enumerate(UNITS):
                    tile = i * TB + UO[u]
                    sp.wait_ge(o_added[u], i + (L * NI + 2))
                    sp.dma_start(out[:, bass.ds(tile * D, w * D)].rearrange("p (t d) -> p t d", d=D),
                                 out_acc[:, bass.ds(tile, w), :]).then_inc(s_out, 16)
            sp.wait_ge(s_out, 16 * 2 * NI)

        @block.gpsimd
        def _(g):
            for q in range(CB):
                g.memset(attr[q][:, :], 1.0).then_inc(s_const, 1)
            g.memset(ident[:, :], 0.0).then_inc(s_const, 1)
            g.iota(iota_i[:, :], pattern=[[1, WIN]], base=0, channel_multiplier=0).then_inc(s_const, 1)
            g.wait_ge(s_const, CB + 2)
            g.affine_select(out=ident[:, :], in_=ident[:, :], compare_op=ALU.not_equal, fill=1.0, base=0,
                            pattern=[[-1, P]], channel_multiplier=1).then_inc(s_const, 1)
            g.iota(ends_i[:, :], pattern=[[TB * P, NI]], base=TB * P, channel_multiplier=0).then_inc(s_const, 1)
            g.memset(node_stop[:, 0:1], 0.0).then_inc(s_const, 1)
            g.memset(agg_t[:, NP:NP + WIN], 0.0).then_inc(s_const, 1)
            g.memset(eps1[:, L:L + 1], 0.0).then_inc(s_const, 1)
            g.memset(lneps[:, :], 1e-5).then_inc(s_const, 1)
            for u in range(2):
                g.sem_inc(stored[u], 16)
            g.wait_ge(s_par, 16 * N_PAR)
            g.wait_ge(s_fill, 32)
            with g.Fori(0, NI) as i:
                for u, w in enumerate(UNITS):
                    acc = out_acc[:, bass.ds(i * TB + UO[u], w), :]
                    g.wait_ge(hn_ready[u], i + 1)
                    g.tensor_tensor(acc, acc, outb[:, :].unsqueeze(1).broadcast_to([P, w, D]), ALU.add)\
                     .then_inc(outb_added[u], 1)
            g.wait_ge(s_ready, 1)

            def gather(dst, index):
                return g.indirect_dma_start(dst, None, h_table, bass.IndirectOffsetOnAxis(ap=index, axis=0))

            def far_pass():
                with g.Fori(0, NG):
                    take(g, f_idx, 16)
                    for j in range(TG):
                        gather(rows[:, 0, j, :], idx[0][:, j:j + 1]).then_inc(f_rows, 16)
                    g.wait_ge(f_rows, 16 * TG)
                    g.inc_swdge_sem([f_rows], [16 * TG], mode="sub")
                    g.sem_inc(f_got, 1)

            with g.Fori(0, L) as l:
                for u in range(2):
                    g.wait_ge(stored[u], l * (NI * 16) + (NI + 1) * 16)
                g.sem_inc(s_passed[g.engine], 1)
                with g.Fori(0, NB) as b:
                    n = l * NB + b
                    for q in range(CB):
                        g.wait_ge(idx_in[q], n * 16 + 16)
                        wait_apart(g, msg_ready, n * GB + (q + 1) * GC)
                        for k in range(GC):
                            for j in range(TG):
                                t = k * TG + j
                                gather(rows[:, q, t, :], idx[q][:, t:t + 1]).then_inc(gathered[q][k], 16)
                far_passes(g, far_pass)

        @block.scalar
        def _(act):
            act.sem_inc(msg_ready, GB)
            for u in range(2):
                act.sem_inc(hid_ready[u], HC)
                act.sem_inc(h_ready[u], 1)
            act.wait_ge(s_const, CB + 8)
            act.wait_ge(s_par, 16 * N_PAR)
            def store(u, i, n, ph):
                act.wait_ge(rows_ready[u], n + 2)
                act.dma_start(h_rows[:, bass.ds(ph % 2 * NT + i * TB + UO[u], UNITS[u]), :], h_n[u][:, :, :])\
                   .then_inc(stored[u], 16)

            def take_h(u, n, func, bias):
                act.wait_ge(h_done[u], n + 1)
                act.wait_ge(o_done[u], n + 1)
                wait_apart(act, seeded[u], n + 1)
                nc.scalar.activation(h_t[u][:, :], h_ps[:, 0:UNITS[u] * P], func, bias=bias)\
                  .then_inc(h_ready[u], 1)

            for half in range(2):
                act.wait_ge(s_var, half + 1)
                cols = slice(half * NT // 2, (half + 1) * NT // 2)
                nc.scalar.activation(std[:, cols], var[:, cols], ACT.Sqrt, bias=lneps[:, 0:1]).then_inc(s_std, 1)
                act.wait_ge(s_norm, half + 1)
                with act.Fori(half * NI // 2, (half + 1) * NI // 2) as i:
                    for u, w in enumerate(UNITS):
                        for j in range(w):
                            t = i * TB + (UO[u] + j)
                            last = nc.scalar.activation(
                                hn[u][:, j:j + 1, :], out_acc[:, bass.ds(t, 1), :], ACT.Relu,
                                bias=nmr[:, bass.ds(t, 1)], scale=rstd[:, bass.ds(t, 1)])
                        last.then_inc(hn_ready[u], 1)
                    for u in range(2):
                        take_h(u, i, ACT.Identity, encb[:, 0:1])
                    for u in range(2):
                        store(u, i, i, 0)
            act.wait_ge(s_ready, 1)

            def far_pass():
                with act.Fori(0, NG):
                    take(act, f_sum, 1)
                    nc.scalar.activation(msg[0][:, :, :], rows[:, 0, 0:TG, :], ACT.Relu).then_inc(f_msg, 1)

            with act.Fori(0, L) as l:

                def node_body(i):
                    n = l * NI + i
                    for u, w in enumerate(UNITS):
                        for c in range(HC):
                            wait_apart(act, z_done[u], n * HC + (c + 1))
                            nc.scalar.activation(hid[u][:, c, :], z_ps[c][:, 0:w * P], ACT.Relu,
                                                 bias=b1s[:, bass.ds(l * HC + c, 1)]).then_inc(hid_ready[u], 1)
                    for u in range(2):
                        take_h(u, n + NI, ACT.Relu, b2s[:, bass.ds(l, 1)])
                    for u in range(2):
                        store(u, i, n + NI, l + 1)

                with act.Fori(0, NB) as b:
                    nodes_before(act, b, node_body)
                    n = l * NB + b
                    for k in range(GB):
                        q, t = k // GC, k % GC * TG
                        act.wait_ge(summed, n * GB + (k + 1 + GB))
                        act.wait_ge(agg_done, n * GB + (k + 1))
                        nc.scalar.activation(msg[k % 2][:, :, :], rows[:, q, t:t + TG, :], ACT.Relu)\
                          .then_inc(msg_ready, 1)
                far_passes(act, far_pass)
                nodes_left(act, node_body)
            for u in range(2):
                act.wait_ge(stored[u], (L + 1) * NI * 16 + 16)

        @block.tensor
        def _(pe):
            pe.sem_inc(agg_done, 2)
            for u in range(2):
                pe.sem_inc(o_done[u], 1)
            pe.wait_ge(s_const, CB + 8)
            pe.wait_ge(s_par, 16 * N_PAR)

            def publish(u, n, ph):
                w = UNITS[u]
                pe.wait_ge(h_ready[u], n + 2)
                if u == 1:
                    pe.wait_ge(rows_ready[0], n + 2)
                for j in range(w):
                    last = nc.tensor.transpose(tr_ps[:, j * P:(j + 1) * P], h_t[u][:, j * P:(j + 1) * P], ident[:, :])
                last.then_inc(tr_done[u], 1)
                pe.wait_ge(o_added[1 - u], n + 1 if u == 0 else n + 2)
                for j in range(w):
                    last = nc.tensor.matmul(o_ps[:, j * P:(j + 1) * P], h_t[u][:, j * P:(j + 1) * P],
                                            outw[:, bass.ds(ph, 1), :].rearrange("p a n -> p (a n)"),
                                            start=True, stop=True)
                last.then_inc(o_done[u], 1)

            with pe.Fori(0, NI) as i:
                pe.wait_ge(rows_ready[1], i + 1)
                for u, w in enumerate(UNITS):
                    pe.wait_ge(hn_ready[u], i + 1)
                    pe.wait_ge(hn_moved[u], i + 1)
                    for j in range(w):
                        last = nc.tensor.transpose(z_ps[u][:, j * P:(j + 1) * P], hn[u][:, j, :], ident[:, :])
                    last.then_inc(hn_turned[u], 1)
                for u, w in enumerate(UNITS):
                    pe.wait_ge(hn_moved[u], i + 2)
                    pe.wait_ge(h_ready[1 - u], i + 1 + u)
                    nc.tensor.matmul(h_ps[:, 0:w * P], encw[:, :], hid[u][:, 0, :], start=True, stop=True)\
                      .then_inc(h_done[u], 1)
                for u in range(2):
                    publish(u, i, 0)
            pe.wait_ge(s_ready, 1)

            def edge_terms(dst, cols, l):
                for j in range(TG):
                    last = nc.tensor.matmul(dst[:, j * D:(j + 1) * D], cols[:, j * P:(j + 1) * P],
                                            edgew[:, bass.ds(l, 1), :].rearrange("p a n -> p (a n)"),
                                            start=True, stop=True)
                return last

            def window_sums(dst, m, hot_m):
                for j in range(TG):
                    last = nc.tensor.matmul(dst[:, 0:WIN], m[:, j, :], hot_m[:, j, :],
                                            start=(j == 0), stop=(j == TG - 1))
                return last

            with pe.Fori(0, L) as l:

                def far_pass():
                    with pe.Fori(0, NG):
                        take(pe, f_attr, 16)
                        edge_terms(e_ps[0], attr[0], l).then_inc(f_e, 1)
                        take(pe, f_hot, 1)
                        take(pe, f_msg, 1)
                        window_sums(agg_ps[0], msg[0], onehot[0]).then_inc(f_agg, 1)

                def node_body(i):
                    n = l * NI + i
                    pe.wait_ge(rows_ready[1], n + NI + 1)
                    for u, w in enumerate(UNITS):
                        cols = agg_t[:, bass.ds((i * TB + UO[u]) * P, w * P)]
                        for c in range(HC):
                            pe.wait_ge(hid_ready[1 - u], n * HC + (c + 1 + u * HC))
                            nc.tensor.matmul(z_ps[c][:, 0:w * P], w1s[:, c * D:(c + 1) * D], cols,
                                             start=True, stop=True).then_inc(z_done[u], 1)
                    for u, w in enumerate(UNITS):
                        pe.wait_ge(h_ready[1 - u], n + (NI + 1 + u))
                        for c in range(HC):
                            pe.wait_ge(hid_ready[u], n * HC + (c + 1 + HC))
                            last = nc.tensor.matmul(h_ps[:, 0:w * P], w2s[:, c, :], hid[u][:, c, :],
                                                    start=(c == 0), stop=(c == HC - 1))
                        last.then_inc(h_done[u], 1)
                    for u in range(2):
                        publish(u, n + NI, l + 1)

                def node_body_between(i, adds):
                    wait_apart(pe, added, adds)
                    node_body(i)

                wait_apart(pe, s_w, l * 32 + 32)
                with pe.Fori(0, NB) as b:
                    n = l * NB + b
                    nodes_before(pe, b, lambda i: node_body_between(i, n * GB + 2))

                    def sums(k):
                        pe.wait_ge(msg_ready, n * GB + (k + 1 + GB))
                        pe.wait_ge(hot, n * GB + (k + 1))
                        pe.wait_ge(added, n * GB + (k + 1))
                        window_sums(agg_ps[k % 2], msg[k % 2], onehot[k % 2]).then_inc(agg_done, 1)

                    for k in range(GB):
                        q, t = k // GC, k % GC * TG
                        if k % GC == 0:
                            wait_apart(pe, attr_in[q], n * 16 + 16)
                        wait_apart(pe, summed, n * GB + (k + GB - 1))
                        edge_terms(e_ps[k % 2], attr[q][:, t * P:(t + TG) * P], l).then_inc(e_done, 1)
                        if k:
                            sums(k - 1)
                    sums(GB - 1)
                far_passes(pe, far_pass)
                wait_apart(pe, agg_all, l + 1)
                nodes_left(pe, node_body)

        @block.vector
        def _(dve):
            dve.sem_inc(summed, GB)
            dve.sem_inc(added, 2)
            for u in range(2):
                dve.sem_inc(hn_moved[u], 1)
                dve.sem_inc(seeded[u], 1)
                dve.sem_inc(rows_ready[u], 1)
                dve.sem_inc(o_added[u], 1)
            v = nc.vector
            step = [0]

            def own(ins):
                step[0] += 1
                ins.then_inc(s_cpy, 1)
                dve.wait_ge(s_cpy, step[0])

            dve.wait_ge(s_dst, 16)
            own(v.tensor_reduce(lo[:, 0, :], dst_n[:, :, :], AX.X, ALU.min))
            own(v.tensor_reduce(lo[:, 1, :], dst_n[:, :, :], AX.X, ALU.max))
            own(v.tensor_tensor(span[:, :], lo[:, 1, :], lo[:, 0, :], ALU.subtract))
            own(v.tensor_copy(spans_i[:, 0, :], lo[:, 0, :]))
            v.tensor_copy(spans_i[:, 1, :], span[:, :]).then_inc(s_span, 1)
            dve.wait_ge(s_src, 16)
            v.tensor_scalar(src_up, src_i, float(NP), None, ALU.add).then_inc(s_src_up, 1)

            def body_stats(i):
                for j in range(TB):
                    t = i * TB + j
                    last = v.bn_stats(stats[:, bass.ds(t, 1), :].rearrange("p a s -> p (a s)"),
                                      out_acc[:, bass.ds(t, 1), :].rearrange("p a d -> p (a d)"))
                last.then_inc(s_stats, 1)

            def moments(half):
                dve.wait_ge(s_stats, (half + 1) * NI // 2)
                c = slice(half * NT // 2, (half + 1) * NT // 2)
                own(v.tensor_tensor(dif[:, c], stats[:, c, 1], stats[:, c, 4], ALU.subtract))
                own(v.tensor_tensor(dif[:, c], dif[:, c], dif[:, c], ALU.mult))
                own(v.tensor_tensor(vs[:, c], stats[:, c, 2], stats[:, c, 5], ALU.add))
                own(v.tensor_scalar(vs[:, c], vs[:, c], 1.0 / D, None, ALU.mult))
                v.scalar_tensor_tensor(out=var[:, c], in0=dif[:, c], scalar=0.25, in1=vs[:, c], op0=ALU.mult,
                                       op1=ALU.add).then_inc(s_var, 1)
                own(v.tensor_tensor(mean[:, c], stats[:, c, 1], stats[:, c, 4], ALU.add))
                dve.wait_ge(s_std, half + 1)
                own(v.reciprocal(rstd[:, c], std[:, c]))
                v.scalar_tensor_tensor(out=nmr[:, c], in0=mean[:, c], scalar=-0.5, in1=rstd[:, c], op0=ALU.mult,
                                       op1=ALU.mult).then_inc(s_norm, 1)

            dve.wait_ge(s_x[0], 16)
            with dve.Fori(0, NI // 2) as i:
                body_stats(i)
            moments(0)
            def publish(u, i, n, ph, first=False):
                w = UNITS[u]
                tile = i * TB + UO[u]
                dve.wait_ge(h_ready[u], n + 2)
                v.tensor_scalar(agg_t[:, bass.ds(tile * P, w * P)], h_t[u][:, :], eps1[:, bass.ds(ph, 1)], None,
                                ALU.mult).then_inc(seeded[u], 1)
                dve.wait_ge(tr_done[u], n + 1)
                dve.wait_ge(stored[u], n * 16 + 16)
                v.tensor_copy(h_n[u][:, :, :], tr_ps[:, 0:w * P].rearrange("p (t d) -> p t d", d=D))\
                 .then_inc(rows_ready[u], 1)
                dve.wait_ge(o_done[u], n + 2)
                if first:
                    dve.wait_ge(outb_added[u], n + 1)
                acc = out_acc[:, bass.ds(tile, w), :]
                v.tensor_tensor(acc, o_ps[:, 0:w * P].rearrange("p (t d) -> p t d", d=D), acc, ALU.add)\
                 .then_inc(o_added[u], 1)

            def encoder_body(i):
                for u, w in enumerate(UNITS):
                    dve.wait_ge(hn_turned[u], i + 1)
                    v.tensor_copy(hid[u][:, 0, :], z_ps[u][:, 0:w * P]).then_inc(hn_moved[u], 1)
                for u in range(2):
                    publish(u, i, i, 0, first=True)

            dve.wait_ge(s_const, CB + 8)
            dve.wait_ge(s_par, 16 * N_PAR)
            own(v.tensor_scalar(eps1[:, :], eps1[:, :], 1.0, None, ALU.add))
            dve.wait_ge(s_x[1], 16)
            with dve.Fori(0, NI // 2) as i:
                body_stats(i + NI // 2)
                encoder_body(i)
            moments(1)
            with dve.Fori(NI // 2, NI) as i:
                encoder_body(i)
            own(v.tensor_copy(iota[:, :], iota_i[:, :]))
            own(v.tensor_copy(ends[:, :], ends_i[:, :]))
            dve.wait_ge(s_sp_in, 64)
            dve.wait_ge(s_dst_t, 16)
            own(v.tensor_tensor(dst_rel[:, :].rearrange("p (g t) -> p g t", t=TG),
                                dst_i[:, :].rearrange("p (g t) -> p g t", t=TG),
                                base_all[:, :].unsqueeze(2).broadcast_to([P, NG, TG]), ALU.subtract))
            own(v.tensor_copy(dst_far[:, :], dst_rel[:, :]))
            own(v.tensor_reduce(span_max[:, :], span_row[:, :], AX.X, ALU.max))
            own(v.tensor_single_scalar(extra[:, :], span_max[:, :], WIN.bit_length() - 1, ALU.arith_shift_right))
            cur = 0
            own(v.tensor_reduce(later_lo[cur][:, :], base_row[:, :].rearrange("a (b g) -> a b g", g=GB), AX.X, ALU.min))
            reach = 1
            while reach < NB:
                own(v.tensor_tensor(later_lo[1 - cur][:, 0:NB - reach], later_lo[cur][:, 0:NB - reach],
                                    later_lo[cur][:, reach:NB], ALU.min))
                own(v.tensor_copy(later_lo[1 - cur][:, NB - reach:NB], later_lo[cur][:, NB - reach:NB]))
                cur, reach = 1 - cur, 2 * reach
            own(v.tensor_tensor(below, later_lo[cur][:, :].unsqueeze(2).broadcast_to([1, NB, NI]),
                                ends[:, :].unsqueeze(1).broadcast_to([1, NB, NI]), ALU.is_ge))
            own(v.tensor_reduce(stop_f[:, :], below, AX.X, ALU.add))
            own(v.tensor_scalar(no_far[:, :], extra[:, :], 0.0, None, ALU.is_equal))
            own(v.tensor_scalar(node_stop[:, 1:NB + 1], stop_f[:, :], no_far[:, 0:1], None, ALU.mult))
            dve.sem_inc(s_ready, 1)



            def one_hot(dst, rel, g):
                return v.tensor_tensor(dst[:, :, :], iota[:, :].unsqueeze(1).broadcast_to([P, TG, WIN]),
                                       rel[:, bass.ds(g * TG, TG)].unsqueeze(2).broadcast_to([P, TG, WIN]),
                                       ALU.is_equal)

            def load_base(table, g):
                return dve.value_load(table[0:1, bass.ds(g, 1)], min_val=0, max_val=NP)

            def add_window(base, ps):
                cols = agg_t[:, bass.ds(base, WIN)]
                return v.tensor_tensor(cols, ps[:, 0:WIN], cols, ALU.add)

            def far_pass():
                v.tensor_scalar(dst_far[:, :], dst_far[:, :], float(WIN), None, ALU.subtract).then_inc(f_shift, 1)
                v.tensor_scalar(far_row[:, :], far_row[:, :], float(WIN), float(NP), ALU.add, ALU.min)\
                 .then_inc(f_shift, 1)
                take(dve, f_shift, 2)
                with dve.Fori(0, NG) as g:
                    dve.sem_inc(f_next, 1)
                    one_hot(onehot[0], dst_far, g).then_inc(f_hot, 1)
                    take(dve, f_e, 1)
                    take(dve, f_got, 1)
                    v.tensor_tensor(rows[:, 0, 0:TG, :], e_ps[0][:, :].rearrange("p (t d) -> p t d", d=D),
                                    rows[:, 0, 0:TG, :], ALU.add).then_inc(f_sum, 1)
                    base = load_base(far_row, g)
                    take(dve, f_agg, 1)
                    add_window(base, agg_ps[0]).then_inc(f_add, 1)
                    take(dve, f_add, 1)

            with dve.Fori(0, L) as l:
                for u in range(2):
                    wait_apart(dve, seeded[u], l * NI + (NI + 1))
                def node_body(i):
                    for u in range(2):
                        publish(u, i, l * NI + i + NI, l + 1)

                with dve.Fori(0, NB) as b:
                    nodes_before(dve, b, node_body)
                    n = l * NB + b

                    def accumulate(k):
                        base = load_base(base_row, b * GB + k)
                        dve.wait_ge(agg_done, n * GB + (k + 3))
                        dve.wait_ge(added, n * GB + (k + 2))
                        add_window(base, agg_ps[k % 2]).then_inc(added, 1)

                    for k in range(GB):
                        q, t = k // GC, k % GC * TG
                        dve.wait_ge(agg_done, n * GB + (k + 1))
                        one_hot(onehot[k % 2], dst_rel, b * GB + k).then_inc(hot, 1)
                        dve.wait_ge(e_done, n * GB + (k + 1))
                        dve.wait_ge(gathered[q][k % GC], n * (16 * TG) + 16 * TG)
                        part = rows[:, q, t:t + TG, :]
                        v.tensor_tensor(part, e_ps[k % 2][:, :].rearrange("p (t d) -> p t d", d=D), part, ALU.add)\
                         .then_inc(summed, 1)
                        if k:
                            accumulate(k - 1)
                    accumulate(GB - 1)
                wait_apart(dve, added, l * NG + (NG + 2))
                far_passes(dve, far_pass)
                dve.sem_inc(agg_all, 1)
                v.tensor_copy(dst_far[:, :], dst_rel[:, :]).then_inc(f_shift, 1)
                v.tensor_copy(far_row[:, :], base_row[:, :]).then_inc(f_shift, 1)
                take(dve, f_shift, 2)
                nodes_left(dve, node_body)


def _layout(a, tiles_up_to):
    import numpy as np

    n = a.shape[0]
    rows = -(-n // (P * tiles_up_to)) * P * tiles_up_to
    padded = np.zeros((rows, *a.shape[1:]), a.dtype)
    padded[:n] = a
    return np.ascontiguousarray(np.moveaxis(padded.reshape(-1, P, *a.shape[1:]), 0, 1)).reshape(P, -1)


def kernel(x, src, dst, edge_attr_16, L0_gnn_enc_w, L0_gnn_enc_b, L0_gnn_edge_w, L0_gnn_edge_b, L0_gnn_mlp_w1,
           L0_gnn_mlp_b1, L0_gnn_mlp_w2, L0_gnn_mlp_b2, L0_gnn_eps, L0_gnn_out_w, L0_gnn_out_b):
    import numpy as np
    import concourse.bacc as bacc
    from concourse.bass_utils import run_bass_kernel_spmd

    x, src, dst, ea = (np.asarray(a) for a in (x, src, dst, edge_attr_16))
    n, e = x.shape[0], src.shape[0]
    ep = -(-e // (P * TC * CB)) * P * TC * CB
    dst_p = np.full(ep, n, dst.dtype)
    dst_p[:e] = dst
    ea_p = np.zeros((KE, ep), ea.dtype)
    ea_p[:, :e] = ea.T
    arrays = {
        "x_t": _layout(x, TB),
        "src_t": _layout(src, TC * CB),
        "dst_t": _layout(dst_p, TC * CB),
        "dst_g": dst_p.reshape(-1, P * TG * GR),
        "ea_t": ea_p,
        "enc_w": np.asarray(L0_gnn_enc_w),
        "enc_b": np.asarray(L0_gnn_enc_b).reshape(D, 1),
        "edge_w": np.asarray(L0_gnn_edge_w),
        "edge_b": np.asarray(L0_gnn_edge_b),
        "w1": np.asarray(L0_gnn_mlp_w1),
        "b1": np.ascontiguousarray(np.asarray(L0_gnn_mlp_b1).reshape(-1, D).T),
        "w2": np.asarray(L0_gnn_mlp_w2),
        "b2": np.ascontiguousarray(np.asarray(L0_gnn_mlp_b2).T),
        "eps": np.asarray(L0_gnn_eps),
        "out_w": np.asarray(L0_gnn_out_w),
        "out_b": np.asarray(L0_gnn_out_b),
    }
    nc = bacc.Bacc("TRN2", target_bir_lowering=False, num_devices=1)
    args = {k: nc.dram_tensor(k, a.shape, mybir.dt.from_np(a.dtype), kind="ExternalInput").ap()
            for k, a in arrays.items()}
    args["out"] = nc.dram_tensor("out", arrays["x_t"].shape, mybir.dt.float32, kind="ExternalOutput").ap()
    gnn_kernel(nc, **args)
    r = run_bass_kernel_spmd(nc, [arrays], core_ids=[0])
    got = r.results[0]["out"].reshape(P, -1, D)
    return np.moveaxis(got, 1, 0).reshape(-1, D)[:n]
```

```python
import concourse.bass as bass
from concourse import mybir
from contextlib import ExitStack

P = 128
D = 128
KE = 16
WIN = 64
TG = 4
GC = 2
CB = 4
TC = TG * GC
GB = GC * CB
GR = 4
UNITS = (4, 3)
TB = sum(UNITS)


def gnn_kernel(nc, x_t, src_t, dst_t, dst_g, ea_t, enc_w, enc_b, edge_w, edge_b, w1, b1, w2, b2,
               eps, out_w, out_b, out, edges):
    f32, i32 = mybir.dt.float32, mybir.dt.int32
    ALU, ACT, AX = mybir.AluOpType, mybir.ActivationFunctionType, mybir.AxisListType

    NT = x_t.shape[1] // D
    NP = NT * P
    NI = NT // TB
    NTE = src_t.shape[1]
    NB = NTE // (TC * CB)
    NCH = NB * CB
    NG = NCH * GC
    SPARE = NTE - -(-edges // P)
    L = w1.shape[0]
    HC = w1.shape[2] // D
    UO = (0, UNITS[0])
    PARTS = (*range(0, NI, 2), NI)
    assert NT % TB == 0 and NTE % (TC * CB) == 0 and NG <= P * GR and HC == 2 and NI > 4

    h_table = nc.dram_tensor("h_table", (2 * NP, D), f32).ap()
    src_l = nc.dram_tensor("src_l", (L, P, NTE), i32).ap()
    h_rows = h_table.rearrange("(t p) d -> p t d", p=P)
    spans_dram = nc.dram_tensor("spans", (2, NG), i32).ap()

    ctx = ExitStack()
    with ctx:
        def sb(name, shape, dt=f32):
            return ctx.enter_context(nc.sbuf_tensor(name, shape, dt))

        def sem(name):
            return ctx.enter_context(nc.semaphore(name))

        def sems(name, n):
            return [sem(f"{name}{i}") for i in range(n)]

        out_acc = sb("out_acc", [P, NT, D])
        agg_t = sb("agg_t", [P, NP + WIN])
        rows = sb("rows", [P, CB, TC, D])
        msg = [sb(f"msg{i}", [P, TG, D]) for i in range(2)]
        onehot = [sb(f"onehot{i}", [P, TG, WIN]) for i in range(2)]
        attr = [sb(f"attr{i}", [KE + 1, TC * P]) for i in range(CB)]
        idx = [sb(f"idx{i}", [P, TC], i32) for i in range(CB)]
        dst_rel = sb("dst_rel", [P, NTE])
        dst_far = sb("dst_far", [P, NTE])
        dst_i = sb("dst_i", [P, NTE], i32)
        dst_n = sb("dst_n", [NG // GR, GR, TG * P], i32)
        lo = sb("lo", [NG // GR, 2, GR])
        span = sb("span", [NG // GR, GR])
        spans_i = sb("spans_i", [NG // GR, 2, GR], i32)
        base_row = sb("base_row", [1, NG], i32)
        far_row = sb("far_row", [1, NG], i32)
        span_row = sb("span_row", [1, NG], i32)
        base_all = sb("base_all", [P, NG], i32)
        span_max = sb("span_max", [1, 1], i32)
        src_i = dst_far[:, :].bitcast(i32)
        later_lo = [sb(f"later_lo{i}", [1, 2 * NB]) for i in range(2)]
        ends_i = sb("ends_i", [1, NI], i32)
        ends = sb("ends", [1, NI])
        below = dst_n[0:1, :, :].rearrange("a g e -> a (g e)").bitcast(f32)[:, 0:NB * NI]\
            .rearrange("a (b i) -> a b i", i=NI)
        no_far = sb("no_far", [1, 1])
        stop_f = sb("stop_f", [1, NB])
        node_stop = sb("node_stop", [1, NB + 1], i32)
        extra = sb("extra", [1, 1], i32)
        iota_i = sb("iota_i", [P, WIN], i32)
        iota = sb("iota", [P, WIN])
        ident = sb("ident", [P, P])
        encw = sb("encw", [P, D])
        encb = sb("encb", [P, 1])
        edgew = sb("edgew", [KE + 1, L, D])
        w1s = sb("w1s", [P, HC * D])
        w2s = sb("w2s", [P, HC, D])
        b1s = sb("b1s", [P, L * HC])
        b2s = sb("b2s", [P, L])
        outw = sb("outw", [P, L + 1, D])
        outb = sb("outb", [P, D])
        eps1 = sb("eps1", [P, L + 1])
        lneps = sb("lneps", [P, 1])
        first_root = sb("first_root", [P, 1])
        stats = sb("stats", [P, NT, 6])
        mean = sb("mean", [P, NT])
        dif = sb("dif", [P, NT])
        var = sb("var", [P, NT])
        vs = sb("vs", [P, NT])
        std = sb("std", [P, NT])
        rstd = sb("rstd", [P, NT])
        nmr = sb("nmr", [P, NT])
        hn = [sb(f"hn{u}", [P, n, D]) for u, n in enumerate(UNITS)]
        hid = [sb(f"hid{u}", [P, HC, n * P]) for u, n in enumerate(UNITS)]
        h_t = [sb(f"h_t{u}", [P, n * P]) for u, n in enumerate(UNITS)]
        h_n = [sb(f"h_n{u}", [P, n, D]) for u, n in enumerate(UNITS)]

        bank = [ctx.enter_context(nc.psum_tensor(f"bank{i}", [P, 512], f32)) for i in range(8)]
        e_ps, agg_ps = bank[0:2], bank[2:4]
        z_ps, h_ps = bank[4:6], bank[6:8]
        turn_ps = e_ps
        o0_ps = [bank[(i + 2) % 8:][:2] for i in range(0, 8, 2)]
        tr_ps, o_ps = z_ps, h_ps
        src_up = rows[:, :, :, :].rearrange("p q t d -> p (q t d)").bitcast(i32)[:, 0:NTE]

        s_par = sem("s_par")
        s_x = sems("s_x", len(PARTS) - 1)
        s_dst = sem("s_dst")
        s_dst_t = sem("s_dst_t")
        s_span = sem("s_span")
        s_sp_out = sem("s_sp_out")
        s_sp_in = sem("s_sp_in")
        s_const = sem("s_const")
        s_step = sem("s_step")
        s_ready = sem("s_ready")
        s_src = sem("s_src")
        s_src_up = sem("s_src_up")
        s_fill = sem("s_fill")
        s_src_out = sem("s_src_out")
        s_var = sem("s_var")
        s_std = sem("s_std")
        s_stats = sem("s_stats")
        s_norm = sem("s_norm")
        hn_ready = sems("hn_ready", 2)
        hn_last = sems("hn_last", 2)
        hn_turned = sems("hn_turned", 2)
        hn_moved = sems("hn_moved", 2)
        outb_added = sems("outb_added", 2)
        z_done = sems("z_done", 2)
        hid_ready = sems("hid_ready", 2)
        h_done = sems("h_done", 2)
        h_ready = sems("h_ready", 2)
        h_kept = sems("h_kept", 2)
        seeded = sems("seeded", 2)
        tr_done = sems("tr_done", 2)
        o_done = sems("o_done", 2)
        rows_ready = sems("rows_ready", 2)
        stored = sems("stored", 2)
        o_added = sems("o_added", 2)
        s_w = sem("s_w")
        idx_in = sems("idx_in", CB)
        attr_in = sems("attr_in", CB)
        gathered = [sems(f"gathered{q}_", GC) for q in range(CB)]
        e_done = sem("e_done")
        hot = sem("hot")
        summed = sem("summed")
        msg_ready = sem("msg_ready")
        agg_done = sem("agg_done")
        added = sem("added")
        f_next, f_idx, f_attr, f_rows, f_got, f_e, f_hot, f_sum, f_msg, f_agg, f_add, f_shift, f_all = (
            sem(n) for n in ("f_next", "f_idx", "f_attr", "f_rows", "f_got", "f_e", "f_hot", "f_sum", "f_msg",
                             "f_agg", "f_add", "f_shift", "f_all"))
        s_out = sem("s_out")
        s_passed = {eng.engine: sem(f"s_passed_{name}") for name, eng in (
            ("pool", nc.gpsimd), ("act", nc.scalar), ("pe", nc.tensor), ("dve", nc.vector))}

        N_PAR = 9
        block = ctx.enter_context(nc.Block())

        def take(eng, s, n):
            eng.wait_ge(s, n)
            eng.sem_clear(s)

        def wait_apart(eng, s, n):
            eng.wait_ge(s, n)
            eng.sem_inc(s_passed[eng.engine], 1)

        def load_extra(eng):
            eng.wait_ge(s_ready, 1)
            return eng.value_load(extra[0:1, 0:1], min_val=0, max_val=NP // WIN + 1)

        def far_passes(eng, n, one_pass, after=None):
            with eng.If(n > 0):
                with eng.Fori(0, n):
                    one_pass()
                if after:
                    after()

        def nodes_before(eng, b, node_body):
            first = eng.value_load(node_stop[0:1, bass.ds(b, 1)], min_val=0, max_val=NI)
            stop = eng.value_load(node_stop[0:1, bass.ds(b + 1, 1)], min_val=0, max_val=NI)
            with eng.If(first < stop):
                with eng.Fori(first, stop) as i:
                    node_body(i)

        def load_left(eng):
            return eng.value_load(node_stop[0:1, NB:NB + 1], min_val=0, max_val=NI)

        def nodes_left(eng, first, node_body):
            with eng.If(first < NI):
                with eng.Fori(first, NI) as i:
                    node_body(i)

        @block.sync
        def _(sp):
            for part in range(len(PARTS) - 1):
                t = slice(PARTS[part] * TB, PARTS[part + 1] * TB)
                sp.dma_start(out_acc[:, t, :], x_t[:, t.start * D:t.stop * D].rearrange("p (t d) -> p t d", d=D))\
                  .then_inc(s_x[part], 16)
            sp.dma_start(encw[:, :], enc_w).then_inc(s_par, 16)
            sp.dma_start(encb[:, :], enc_b).then_inc(s_par, 16)
            sp.dma_start(edgew[0:KE, :, :], edge_w.rearrange("l k n -> k l n")).then_inc(s_par, 16)
            sp.dma_start(edgew[KE:KE + 1, :, :], edge_b.rearrange("(a l) n -> a l n", a=1)).then_inc(s_par, 16)
            sp.dma_start(b1s[:, :], b1).then_inc(s_par, 16)
            sp.dma_start(b2s[:, :], b2).then_inc(s_par, 16)
            sp.dma_start(outw[:, :, :], out_w.rearrange("(l k) n -> k l n", k=D)).then_inc(s_par, 16)
            sp.dma_start(outb[:, :], out_b.partition_broadcast(P)).then_inc(s_par, 16)
            sp.dma_start(eps1[:, 0:L], eps.partition_broadcast(P)).then_inc(s_par, 16)
            sp.dma_start(dst_n[:, :, :], dst_g.rearrange("c (g e) -> c g e", g=GR)).then_inc(s_dst, 16)
            sp.dma_start(src_i, src_t).then_inc(s_src, 16)
            sp.dma_start(dst_i[:, :], dst_t).then_inc(s_dst_t, 16)
            for l in range(0, L, 2):
                sp.dma_start(src_l[l, :, :], src_t).then_inc(s_src_out, 16)
            sp.wait_ge(s_src_up, 1)
            for l in range(1, L, 2):
                sp.dma_start(src_l[l, :, :], src_up).then_inc(s_src_out, 16)
            sp.wait_ge(s_span, 1)
            for i in range(2):
                sp.dma_start(spans_dram[i, :].rearrange("(c g) -> c g", g=GR), spans_i[:, i, :])\
                  .then_inc(s_sp_out, 16)
            sp.wait_ge(s_sp_out, 32)
            sp.dma_start(base_row[:, :], spans_dram[0:1, :]).then_inc(s_sp_in, 16)
            sp.dma_start(far_row[:, :], spans_dram[0:1, :]).then_inc(s_sp_in, 16)
            sp.dma_start(span_row[:, :], spans_dram[1:2, :]).then_inc(s_sp_in, 16)
            sp.dma_start(base_all[:, :], spans_dram[0, :].partition_broadcast(P)).then_inc(s_sp_in, 16)

            with sp.Fori(0, NI) as i:
                for u, w in enumerate(UNITS):
                    sp.wait_ge(rows_ready[u], i + 2)
                    sp.dma_start(h_rows[:, bass.ds(i * TB + UO[u], w), :], h_n[u][:, :, :]).then_inc(stored[u], 16)
                sp.dma_start(h_rows[:, bass.ds(i * TB + NT, TB), :],
                             x_t[:, bass.ds(i * (TB * D), TB * D)].rearrange("p (t d) -> p t d", d=D))\
                  .then_inc(s_fill, 16)
            sp.wait_ge(s_const, CB)
            sp.wait_ge(s_src_out, 16 * L)
            with sp.Fori(0, L) as l:
                layer_src = src_l[bass.ds(l, 1), :, :].rearrange("a p t -> (a p) t")

                def far_pass():
                    with sp.Fori(0, NG) as g:
                        take(sp, f_next, 1)
                        sp.dma_start(idx[0][:, 0:TG], layer_src[:, bass.ds(g * TG, TG)]).then_inc(f_idx, 16)
                        sp.dma_start(attr[0][0:KE, 0:TG * P], ea_t[:, bass.ds(g * (TG * P), TG * P)])\
                          .then_inc(f_attr, 16)

                for u in range(2):
                    sp.wait_ge(h_ready[u], l * NI + (NI + 1))
                sp.dma_start(w1s[:, :], w1[bass.ds(l, 1), :, :].rearrange("a k n -> (a k) n")).then_inc(s_w, 16)
                sp.dma_start(w2s[:, :, :], w2[bass.ds(l, 1), :, :].rearrange("a (c p) n -> (a p) c n", p=D))\
                  .then_inc(s_w, 16)
                with sp.Fori(0, NB) as b:
                    n = l * NB + b
                    for q in range(CB):
                        c = b * CB + q
                        sp.wait_ge(summed, n * GB + (q + 1) * GC)
                        sp.dma_start(idx[q][:, :], layer_src[:, bass.ds(c * TC, TC)]).then_inc(idx_in[q], 16)
                        sp.dma_start(attr[q][0:KE, :], ea_t[:, bass.ds(c * (TC * P), TC * P)])\
                          .then_inc(attr_in[q], 16)
                far_passes(sp, load_extra(sp), far_pass)
            with sp.Fori(0, NI) as i:
                for u, w in enumerate(UNITS):
                    tile = i * TB + UO[u]
                    sp.wait_ge(o_added[u], i + (L * NI + 2))
                    sp.dma_start(out[:, bass.ds(tile * D, w * D)].rearrange("p (t d) -> p t d", d=D),
                                 out_acc[:, bass.ds(tile, w), :]).then_inc(s_out, 16)
            sp.wait_ge(s_out, 16 * 2 * NI)

        @block.gpsimd
        def _(g):
            for q in range(CB):
                g.memset(attr[q][:, :], 1.0).then_inc(s_const, 1)
            g.memset(ident[:, :], 0.0).then_inc(s_const, 1)
            g.iota(iota_i[:, :], pattern=[[1, WIN]], base=0, channel_multiplier=0).then_inc(s_const, 1)
            g.wait_ge(s_const, CB + 2)
            g.affine_select(out=ident[:, :], in_=ident[:, :], compare_op=ALU.not_equal, fill=1.0, base=0,
                            pattern=[[-1, P]], channel_multiplier=1).then_inc(s_const, 1)
            g.iota(ends_i[:, :], pattern=[[TB * P, NI]], base=TB * P, channel_multiplier=0).then_inc(s_const, 1)
            g.memset(node_stop[:, 0:1], 0.0).then_inc(s_const, 1)
            g.memset(agg_t[:, NP:NP + WIN], 0.0).then_inc(s_const, 1)
            g.memset(eps1[:, L:L + 1], 0.0).then_inc(s_const, 1)
            for i in range(2):
                g.memset(later_lo[i][:, NB:2 * NB], float(2 * NP)).then_inc(s_const, 1)
            g.memset(lneps[:, :], 1e-5).then_inc(s_const, 1)
            for u in range(2):
                g.sem_inc(stored[u], 16)
            g.wait_ge(s_src, 16)
            g.tensor_scalar(src_up, src_i, float(NP), None, ALU.add).then_inc(s_src_up, 1)
            g.wait_ge(s_par, 16 * N_PAR)
            with g.Fori(0, NI) as i:
                for u, w in enumerate(UNITS):
                    acc = out_acc[:, bass.ds(i * TB + UO[u], w), :]
                    g.wait_ge(hn_ready[u], i + 1)
                    g.wait_ge(hn_last[u], i + 1)
                    g.tensor_tensor(acc, acc, outb[:, :].unsqueeze(1).broadcast_to([P, w, D]), ALU.add)\
                     .then_inc(outb_added[u], 1)

            g.wait_ge(s_fill, 16 * NI)

            def gather(dst, index):
                return g.indirect_dma_start(dst, None, h_table, bass.IndirectOffsetOnAxis(ap=index, axis=0))

            def far_pass():
                with g.Fori(0, NG):
                    take(g, f_idx, 16)
                    for j in range(TG):
                        gather(rows[:, 0, j, :], idx[0][:, j:j + 1]).then_inc(f_rows, 16)
                    g.wait_ge(f_rows, 16 * TG)
                    g.inc_swdge_sem([f_rows], [16 * TG], mode="sub")
                    g.sem_inc(f_got, 1)

            with g.Fori(0, L) as l:
                for u in range(2):
                    g.wait_ge(stored[u], l * (NI * 16) + (NI + 1) * 16)
                g.sem_inc(s_passed[g.engine], 1)

                def edge_body(b, spare):
                    n = l * NB + b
                    for q in range(CB):
                        g.wait_ge(idx_in[q], n * 16 + 16)
                        wait_apart(g, msg_ready, n * GB + (q + 1) * GC)
                        for k in range(GC):
                            for j in range(TG):
                                t = k * TG + j
                                if q * TC + t < TC * CB - spare:
                                    gather(rows[:, q, t, :], idx[q][:, t:t + 1]).then_inc(gathered[q][k], 16)
                                else:
                                    g.inc_swdge_sem([gathered[q][k]], [16], mode="add")

                with g.Fori(0, NB - 1) as b:
                    edge_body(b, 0)
                edge_body(NB - 1, SPARE)
                far_passes(g, load_extra(g), far_pass)

        @block.scalar
        def _(act):
            act.sem_inc(msg_ready, GB)
            for u in range(2):
                act.sem_inc(hid_ready[u], HC)
                act.sem_inc(h_ready[u], 1)
            act.wait_ge(s_const, CB + 10)
            nc.scalar.activation(first_root[:, :], lneps[:, :], ACT.Sqrt, bias=lneps[:, 0:1])
            act.wait_ge(s_par, 16 * N_PAR)

            def store(u, i, n, ph):
                act.wait_ge(rows_ready[u], n + 2)
                act.dma_start(h_rows[:, bass.ds(ph % 2 * NT + i * TB + UO[u], UNITS[u]), :], h_n[u][:, :, :])\
                   .then_inc(stored[u], 16)

            def take_h(u, n, l):
                act.wait_ge(h_done[u], n + 1)
                act.wait_ge(o_done[u], n + 1)
                wait_apart(act, seeded[u], n + 1)
                nc.scalar.activation(h_t[u][:, :], h_ps[u][:, 0:UNITS[u] * P], ACT.Relu,
                                     bias=b2s[:, bass.ds(l, 1)]).then_inc(h_ready[u], 1)

            def normalise(i):
                for u, w in enumerate(UNITS):
                    act.wait_ge(hn_turned[u], i + 1)
                    for j in range(w - 1):
                        t = i * TB + (UO[u] + j)
                        last = nc.scalar.activation(
                            hn[u][:, j:j + 1, :], out_acc[:, bass.ds(t, 1), :], ACT.Relu,
                            bias=nmr[:, bass.ds(t, 1)], scale=rstd[:, bass.ds(t, 1)])
                    last.then_inc(hn_ready[u], 1)

            def node_cols(i, u):
                return agg_t[:, bass.ds((i * TB + UO[u]) * P, UNITS[u] * P)]

            def take_h0(i):
                for u, w in enumerate(UNITS):
                    act.wait_ge(h_done[u], i + 1)
                    act.wait_ge(tr_done[u], i + 1)
                    act.wait_ge(h_kept[u], i + 1)
                    nc.scalar.activation(h_t[u][:, :], h_ps[u][:, 0:w * P], ACT.Identity, bias=encb[:, 0:1])\
                      .then_inc(h_ready[u], 1)

            def seed0(i):
                for u in range(2):
                    act.wait_ge(o_done[u], i + 2)
                    nc.scalar.activation(node_cols(i, u), node_cols(i, u), ACT.Identity, scale=eps1[:, 0:1])\
                      .then_inc(seeded[u], 1)

            act.wait_ge(s_var, 1)
            nc.scalar.activation(std[:, :], var[:, :], ACT.Sqrt, bias=lneps[:, 0:1]).then_inc(s_std, 1)
            act.wait_ge(s_norm, 1)
            normalise(0)
            with act.Fori(0, NI - 1) as i:
                normalise(i + 1)
                take_h0(i)
            take_h0(NI - 1)
            with act.Fori(0, NI) as i:
                seed0(i)

            def far_pass():
                with act.Fori(0, NG):
                    take(act, f_sum, 1)
                    nc.scalar.activation(msg[0][:, :, :], rows[:, 0, 0:TG, :], ACT.Relu).then_inc(f_msg, 1)

            n_far = load_extra(act)
            with act.Fori(0, L) as l:

                def node_body(i):
                    n = l * NI + i
                    for u, w in enumerate(UNITS):
                        for c in range(HC):
                            wait_apart(act, z_done[u], n * HC + (c + 1))
                            nc.scalar.activation(hid[u][:, c, :], z_ps[c][:, 0:w * P], ACT.Relu,
                                                 bias=b1s[:, bass.ds(l * HC + c, 1)]).then_inc(hid_ready[u], 1)
                    for u in range(2):
                        take_h(u, n + NI, l)
                    for u in range(2):
                        store(u, i, n + NI, l + 1)

                with act.Fori(0, NB) as b:
                    nodes_before(act, b, node_body)
                    n = l * NB + b
                    for k in range(GB):
                        q, t = k // GC, k % GC * TG
                        act.wait_ge(summed, n * GB + (k + 1 + GB))
                        act.wait_ge(agg_done, n * GB + (k + 1))
                        nc.scalar.activation(msg[k % 2][:, :, :], rows[:, q, t:t + TG, :], ACT.Relu)\
                          .then_inc(msg_ready, 1)
                first = load_left(act)
                far_passes(act, n_far, far_pass)
                nodes_left(act, first, node_body)
            for u in range(2):
                act.wait_ge(stored[u], (L + 1) * NI * 16 + 16)

        @block.tensor
        def _(pe):
            pe.sem_inc(agg_done, 2)
            for u in range(2):
                pe.sem_inc(o_done[u], 1)
                pe.sem_inc(hn_turned[u], 1)
                pe.sem_inc(tr_done[u], 1)
            pe.wait_ge(s_const, CB + 10)
            pe.wait_ge(s_par, 16 * N_PAR)

            def turn_back(n):
                for u, w in enumerate(UNITS):
                    pe.wait_ge(h_ready[u], n + 2)
                    pe.wait_ge(rows_ready[u], n + 1)
                    for j in range(w):
                        last = nc.tensor.transpose(tr_ps[u][:, j * P:(j + 1) * P], h_t[u][:, j * P:(j + 1) * P],
                                                   ident[:, :])
                    last.then_inc(tr_done[u], 1)

            def output_part(u, ph, o_ps, cols):
                for j in range(UNITS[u]):
                    last = nc.tensor.matmul(o_ps[u][:, j * P:(j + 1) * P], cols[:, j * P:(j + 1) * P],
                                            outw[:, bass.ds(ph, 1), :].rearrange("p a n -> p (a n)"),
                                            start=True, stop=True)
                last.then_inc(o_done[u], 1)

            def turn(i):
                for u, w in enumerate(UNITS):
                    pe.wait_ge(hn_ready[u], i + 1)
                    pe.wait_ge(hn_last[u], i + 1)
                    pe.wait_ge(hn_moved[u], i + 1)
                    for j in range(w):
                        last = nc.tensor.transpose(turn_ps[u][:, j * P:(j + 1) * P], hn[u][:, j, :], ident[:, :])
                    last.then_inc(hn_turned[u], 1)

            def encode(i):
                for u, w in enumerate(UNITS):
                    pe.wait_ge(hn_moved[u], i + 2)
                    pe.wait_ge(h_ready[u], i + 1)
                    nc.tensor.matmul(h_ps[u][:, 0:w * P], encw[:, :], hid[u][:, 0, :], start=True, stop=True)\
                      .then_inc(h_done[u], 1)

            turn(0)
            with pe.Fori(0, NI - 1) as i:
                encode(i)
                turn(i + 1)
                turn_back(i)
            encode(NI - 1)
            turn_back(NI - 1)
            for i in range(NI):
                for u, w in enumerate(UNITS):
                    pe.wait_ge(h_kept[u], NI + 1)
                    if i >= len(o0_ps):
                        pe.wait_ge(o_added[u], i - len(o0_ps) + 2)
                    first = (i * TB + UO[u]) * P
                    output_part(u, 0, o0_ps[i % len(o0_ps)], agg_t[:, first:first + w * P])
            for u in range(2):
                pe.wait_ge(o_added[u], NI + 1)

            def edge_terms(dst, cols, l):
                for j in range(TG):
                    last = nc.tensor.matmul(dst[:, j * D:(j + 1) * D], cols[:, j * P:(j + 1) * P],
                                            edgew[:, bass.ds(l, 1), :].rearrange("p a n -> p (a n)"),
                                            start=True, stop=True)
                return last

            def window_sums(dst, m, hot_m):
                for j in range(TG):
                    last = nc.tensor.matmul(dst[:, 0:WIN], m[:, j, :], hot_m[:, j, :],
                                            start=(j == 0), stop=(j == TG - 1))
                return last

            n_far = load_extra(pe)
            with pe.Fori(0, L) as l:

                def far_pass():
                    with pe.Fori(0, NG):
                        take(pe, f_attr, 16)
                        edge_terms(e_ps[0], attr[0], l).then_inc(f_e, 1)
                        take(pe, f_hot, 1)
                        take(pe, f_msg, 1)
                        window_sums(agg_ps[0], msg[0], onehot[0]).then_inc(f_agg, 1)

                def node_body(i):
                    n = l * NI + i
                    for u, w in enumerate(UNITS):
                        cols = agg_t[:, bass.ds((i * TB + UO[u]) * P, w * P)]
                        for c in range(HC):
                            if u == 0:
                                pe.wait_ge(rows_ready[c], n + (NI + 1))
                            else:
                                pe.wait_ge(hid_ready[0], n * HC + (c + 1 + HC))
                            nc.tensor.matmul(z_ps[c][:, 0:w * P], w1s[:, c * D:(c + 1) * D], cols,
                                             start=True, stop=True).then_inc(z_done[u], 1)
                    for u, w in enumerate(UNITS):
                        pe.wait_ge(o_added[u], n + (NI + 1))
                        for c in range(HC):
                            pe.wait_ge(hid_ready[u], n * HC + (c + 1 + HC))
                            last = nc.tensor.matmul(h_ps[u][:, 0:w * P], w2s[:, c, :], hid[u][:, c, :],
                                                    start=(c == 0), stop=(c == HC - 1))
                        last.then_inc(h_done[u], 1)
                    turn_back(n + NI)
                    for u in range(2):
                        output_part(u, l + 1, o_ps, h_t[u])

                def node_body_between(i, adds):
                    wait_apart(pe, added, adds)
                    node_body(i)

                wait_apart(pe, s_w, l * 32 + 32)
                with pe.Fori(0, NB) as b:
                    n = l * NB + b
                    nodes_before(pe, b, lambda i: node_body_between(i, n * GB + 2))

                    def sums(k):
                        pe.wait_ge(msg_ready, n * GB + (k + 1 + GB))
                        pe.wait_ge(hot, n * GB + (k + 1))
                        pe.wait_ge(added, n * GB + (k + 1))
                        window_sums(agg_ps[k % 2], msg[k % 2], onehot[k % 2]).then_inc(agg_done, 1)

                    for k in range(GB):
                        q, t = k // GC, k % GC * TG
                        if k % GC == 0:
                            wait_apart(pe, attr_in[q], n * 16 + 16)
                        wait_apart(pe, summed, n * GB + (k + GB - 1))
                        edge_terms(e_ps[k % 2], attr[q][:, t * P:(t + TG) * P], l).then_inc(e_done, 1)
                        if k:
                            sums(k - 1)
                    sums(GB - 1)
                first = load_left(pe)
                wait_apart(pe, added, l * NG + (NG + 2))
                far_passes(pe, n_far, far_pass, lambda: take(pe, f_all, 1))
                nodes_left(pe, first, node_body)

        @block.vector
        def _(dve):
            dve.sem_inc(summed, GB)
            dve.sem_inc(added, 2)
            for u in range(2):
                dve.sem_inc(hn_moved[u], 1)
                dve.sem_inc(h_kept[u], 1)
                dve.sem_inc(seeded[u], 1)
                dve.sem_inc(rows_ready[u], 1)
                dve.sem_inc(o_added[u], 1)
            v = nc.vector
            step = [0]

            def own(ins):
                step[0] += 1
                ins.then_inc(s_step, 1)
                dve.wait_ge(s_step, step[0])

            dve.wait_ge(s_const, CB + 10)
            own(v.tensor_copy(iota[:, :], iota_i[:, :]))
            own(v.tensor_copy(ends[:, :], ends_i[:, :]))
            for part in range(len(PARTS) - 1):
                dve.wait_ge(s_x[part], 16)
                for t in range(PARTS[part] * TB, PARTS[part + 1] * TB):
                    v.bn_stats(stats[:, t, :], out_acc[:, t, :]).then_inc(s_stats, 1)
            dve.wait_ge(s_stats, NT)
            own(v.tensor_tensor(dif[:, :], stats[:, :, 1], stats[:, :, 4], ALU.subtract))
            own(v.tensor_tensor(dif[:, :], dif[:, :], dif[:, :], ALU.mult))
            own(v.tensor_tensor(vs[:, :], stats[:, :, 2], stats[:, :, 5], ALU.add))
            own(v.tensor_scalar(vs[:, :], vs[:, :], 1.0 / D, None, ALU.mult))
            v.scalar_tensor_tensor(out=var[:, :], in0=dif[:, :], scalar=0.25, in1=vs[:, :], op0=ALU.mult,
                                   op1=ALU.add).then_inc(s_var, 1)
            own(v.tensor_tensor(mean[:, :], stats[:, :, 1], stats[:, :, 4], ALU.add))
            dve.wait_ge(s_std, 1)
            own(v.reciprocal(rstd[:, :], std[:, :]))
            v.scalar_tensor_tensor(out=nmr[:, :], in0=mean[:, :], scalar=-0.5, in1=rstd[:, :], op0=ALU.mult,
                                   op1=ALU.mult).then_inc(s_norm, 1)

            def take_rows(n):
                for u, w in enumerate(UNITS):
                    dve.wait_ge(tr_done[u], n + 2)
                    dve.wait_ge(stored[u], n * 16 + 16)
                    v.tensor_copy(h_n[u][:, :, :], tr_ps[u][:, 0:w * P].rearrange("p (t d) -> p t d", d=D))\
                     .then_inc(rows_ready[u], 1)

            def keep_h0(i):
                for u, w in enumerate(UNITS):
                    dve.wait_ge(h_ready[u], i + 2)
                    v.tensor_copy(agg_t[:, bass.ds((i * TB + UO[u]) * P, w * P)], h_t[u][:, :]).then_inc(h_kept[u], 1)

            def add_output(u, i, n, o_ps):
                dve.wait_ge(o_done[u], n + 2)
                acc = out_acc[:, bass.ds(i * TB + UO[u], UNITS[u]), :]
                v.tensor_tensor(acc, o_ps[u][:, 0:UNITS[u] * P].rearrange("p (t d) -> p t d", d=D), acc, ALU.add)\
                 .then_inc(o_added[u], 1)

            def normalise_last(i):
                for u, w in enumerate(UNITS):
                    t = i * TB + (UO[u] + w - 1)
                    dve.wait_ge(hn_turned[u], i + 1)
                    v.tensor_scalar(hn[u][:, w - 1:w, :], out_acc[:, bass.ds(t, 1), :], rstd[:, bass.ds(t, 1)],
                                    nmr[:, bass.ds(t, 1)], ALU.mult, ALU.add).then_inc(hn_last[u], 1)

            def move_turned(i):
                for u, w in enumerate(UNITS):
                    dve.wait_ge(hn_turned[u], i + 2)
                    v.tensor_scalar(hid[u][:, 0, :], turn_ps[u][:, 0:w * P], 0.0, None, ALU.max)\
                     .then_inc(hn_moved[u], 1)

            dve.wait_ge(s_norm, 1)
            normalise_last(0)
            dve.wait_ge(s_dst, 16)
            v.tensor_reduce(lo[:, 0, :], dst_n[:, :, :], AX.X, ALU.min).then_inc(s_step, 1)
            move_turned(0)
            v.tensor_reduce(lo[:, 1, :], dst_n[:, :, :], AX.X, ALU.max).then_inc(s_step, 1)
            step[0] += 2
            dve.wait_ge(s_step, step[0])
            own(v.tensor_tensor(span[:, :], lo[:, 1, :], lo[:, 0, :], ALU.subtract))
            own(v.tensor_copy(spans_i[:, 0, :], lo[:, 0, :]))
            v.tensor_copy(spans_i[:, 1, :], span[:, :]).then_inc(s_span, 1)
            dve.wait_ge(s_par, 16 * N_PAR)
            own(v.tensor_scalar(eps1[:, :], eps1[:, :], 1.0, None, ALU.add))
            normalise_last(1)
            with dve.Fori(0, NI - 2) as i:
                move_turned(i + 1)
                normalise_last(i + 2)
                take_rows(i)
                keep_h0(i)
            move_turned(NI - 1)
            take_rows(NI - 2)
            keep_h0(NI - 2)
            take_rows(NI - 1)
            keep_h0(NI - 1)
            dve.wait_ge(s_sp_in, 64)
            dve.wait_ge(s_dst_t, 16)
            own(v.tensor_tensor(dst_rel[:, :].rearrange("p (g t) -> p g t", t=TG),
                                dst_i[:, :].rearrange("p (g t) -> p g t", t=TG),
                                base_all[:, :].unsqueeze(2).broadcast_to([P, NG, TG]), ALU.subtract))
            own(v.tensor_copy(dst_far[:, :], dst_rel[:, :]))
            own(v.tensor_reduce(span_max[:, :], span_row[:, :], AX.X, ALU.max))
            own(v.tensor_single_scalar(extra[:, :], span_max[:, :], WIN.bit_length() - 1, ALU.arith_shift_right))
            cur = 0
            own(v.tensor_reduce(later_lo[cur][:, 0:NB], base_row[:, :].rearrange("a (b g) -> a b g", g=GB), AX.X, ALU.min))
            reach = 1
            while reach < NB:
                own(v.tensor_tensor(later_lo[1 - cur][:, 0:NB], later_lo[cur][:, 0:NB],
                                    later_lo[cur][:, reach:NB + reach], ALU.min))
                cur, reach = 1 - cur, 2 * reach
            own(v.tensor_tensor(below, later_lo[cur][:, 0:NB].unsqueeze(2).broadcast_to([1, NB, NI]),
                                ends[:, :].unsqueeze(1).broadcast_to([1, NB, NI]), ALU.is_ge))
            own(v.tensor_reduce(stop_f[:, :], below, AX.X, ALU.add))
            own(v.tensor_scalar(no_far[:, :], extra[:, :], 0.0, None, ALU.is_equal))
            own(v.tensor_scalar(node_stop[:, 1:NB + 1], stop_f[:, :], no_far[:, 0:1], None, ALU.mult))
            dve.sem_inc(s_ready, 1)
            for i in range(NI):
                for u in range(2):
                    dve.wait_ge(outb_added[u], i + 1)
                    add_output(u, i, i, o0_ps[i % len(o0_ps)])



            def one_hot(dst, rel, g):
                return v.tensor_tensor(dst[:, :, :], iota[:, :].unsqueeze(1).broadcast_to([P, TG, WIN]),
                                       rel[:, bass.ds(g * TG, TG)].unsqueeze(2).broadcast_to([P, TG, WIN]),
                                       ALU.is_equal)

            def load_base(table, g):
                return dve.value_load(table[0:1, bass.ds(g, 1)], min_val=0, max_val=NP)

            def add_window(base, ps):
                cols = agg_t[:, bass.ds(base, WIN)]
                return v.tensor_tensor(cols, ps[:, 0:WIN], cols, ALU.add)

            def far_pass():
                v.tensor_scalar(dst_far[:, :], dst_far[:, :], float(WIN), None, ALU.subtract).then_inc(f_shift, 1)
                v.tensor_scalar(far_row[:, :], far_row[:, :], float(WIN), float(NP), ALU.add, ALU.min)\
                 .then_inc(f_shift, 1)
                take(dve, f_shift, 2)
                with dve.Fori(0, NG) as g:
                    dve.sem_inc(f_next, 1)
                    one_hot(onehot[0], dst_far, g).then_inc(f_hot, 1)
                    take(dve, f_e, 1)
                    take(dve, f_got, 1)
                    v.tensor_tensor(rows[:, 0, 0:TG, :], e_ps[0][:, :].rearrange("p (t d) -> p t d", d=D),
                                    rows[:, 0, 0:TG, :], ALU.add).then_inc(f_sum, 1)
                    base = load_base(far_row, g)
                    take(dve, f_agg, 1)
                    add_window(base, agg_ps[0]).then_inc(f_add, 1)
                    take(dve, f_add, 1)

            def windows_back():
                v.tensor_copy(dst_far[:, :], dst_rel[:, :]).then_inc(f_shift, 1)
                v.tensor_copy(far_row[:, :], base_row[:, :]).then_inc(f_shift, 1)
                take(dve, f_shift, 2)
                dve.sem_inc(f_all, 1)

            n_far = load_extra(dve)
            with dve.Fori(0, L) as l:
                for u in range(2):
                    wait_apart(dve, seeded[u], l * NI + (NI + 1))

                def node_body(i):
                    n = l * NI + i + NI
                    take_rows(n)
                    for u, w in enumerate(UNITS):
                        v.tensor_scalar(agg_t[:, bass.ds((i * TB + UO[u]) * P, w * P)], h_t[u][:, :],
                                        eps1[:, bass.ds(l + 1, 1)], None, ALU.mult).then_inc(seeded[u], 1)
                    for u in range(2):
                        add_output(u, i, n, o_ps)

                with dve.Fori(0, NB) as b:
                    nodes_before(dve, b, node_body)
                    n = l * NB + b

                    def accumulate(k):
                        base = load_base(base_row, b * GB + k)
                        dve.wait_ge(agg_done, n * GB + (k + 3))
                        dve.wait_ge(added, n * GB + (k + 2))
                        add_window(base, agg_ps[k % 2]).then_inc(added, 1)

                    for k in range(GB):
                        q, t = k // GC, k % GC * TG
                        dve.wait_ge(agg_done, n * GB + (k + 1))
                        one_hot(onehot[k % 2], dst_rel, b * GB + k).then_inc(hot, 1)
                        dve.wait_ge(e_done, n * GB + (k + 1))
                        dve.wait_ge(gathered[q][k % GC], n * (16 * TG) + 16 * TG)
                        part = rows[:, q, t:t + TG, :]
                        v.tensor_tensor(part, e_ps[k % 2][:, :].rearrange("p (t d) -> p t d", d=D), part, ALU.add)\
                         .then_inc(summed, 1)
                        if k:
                            accumulate(k - 1)
                    accumulate(GB - 1)
                first = load_left(dve)
                wait_apart(dve, added, l * NG + (NG + 2))
                far_passes(dve, n_far, far_pass, windows_back)
                nodes_left(dve, first, node_body)


def _layout(a, tiles_up_to):
    import numpy as np

    n = a.shape[0]
    rows = -(-n // (P * tiles_up_to)) * P * tiles_up_to
    padded = np.zeros((rows, *a.shape[1:]), a.dtype)
    padded[:n] = a
    return np.ascontiguousarray(np.moveaxis(padded.reshape(-1, P, *a.shape[1:]), 0, 1)).reshape(P, -1)


def kernel(x, src, dst, edge_attr_16, L0_gnn_enc_w, L0_gnn_enc_b, L0_gnn_edge_w, L0_gnn_edge_b, L0_gnn_mlp_w1,
           L0_gnn_mlp_b1, L0_gnn_mlp_w2, L0_gnn_mlp_b2, L0_gnn_eps, L0_gnn_out_w, L0_gnn_out_b):
    import numpy as np
    import concourse.bacc as bacc
    from concourse.bass_utils import run_bass_kernel_spmd

    x, src, dst, ea = (np.asarray(a) for a in (x, src, dst, edge_attr_16))
    n, e = x.shape[0], src.shape[0]
    ep = -(-e // (P * TC * CB)) * P * TC * CB
    dst_p = np.full(ep, n, dst.dtype)
    dst_p[:e] = dst
    ea_p = np.zeros((KE, ep), ea.dtype)
    ea_p[:, :e] = ea.T
    arrays = {
        "x_t": _layout(x, TB),
        "src_t": _layout(src, TC * CB),
        "dst_t": _layout(dst_p, TC * CB),
        "dst_g": dst_p.reshape(-1, P * TG * GR),
        "ea_t": ea_p,
        "enc_w": np.asarray(L0_gnn_enc_w),
        "enc_b": np.asarray(L0_gnn_enc_b).reshape(D, 1),
        "edge_w": np.asarray(L0_gnn_edge_w),
        "edge_b": np.asarray(L0_gnn_edge_b),
        "w1": np.asarray(L0_gnn_mlp_w1),
        "b1": np.ascontiguousarray(np.asarray(L0_gnn_mlp_b1).reshape(-1, D).T),
        "w2": np.asarray(L0_gnn_mlp_w2),
        "b2": np.ascontiguousarray(np.asarray(L0_gnn_mlp_b2).T),
        "eps": np.asarray(L0_gnn_eps),
        "out_w": np.asarray(L0_gnn_out_w),
        "out_b": np.asarray(L0_gnn_out_b),
    }
    nc = bacc.Bacc("TRN2", target_bir_lowering=False, num_devices=1)
    args = {k: nc.dram_tensor(k, a.shape, mybir.dt.from_np(a.dtype), kind="ExternalInput").ap()
            for k, a in arrays.items()}
    args["out"] = nc.dram_tensor("out", arrays["x_t"].shape, mybir.dt.float32, kind="ExternalOutput").ap()
    gnn_kernel(nc, **args, edges=e)
    r = run_bass_kernel_spmd(nc, [arrays], core_ids=[0])
    got = r.results[0]["out"].reshape(P, -1, D)
    return np.moveaxis(got, 1, 0).reshape(-1, D)[:n]
```
